# Optimizing a Trainium2 kernel written in Bass

```python
import numpy as np
import jax
import jax.numpy as jnp

def _softmax(x, axis=-1):
    return jax.nn.softmax(x, axis=axis)

def _gelu(x):
    return jax.nn.gelu(x, approximate=True)

def _silu(x):
    return jax.nn.silu(x)

def _sigmoid(x):
    return jax.nn.sigmoid(x)

def _layernorm(x, axis=-1, eps=1e-05):
    m = jnp.mean(x, axis=axis, keepdims=True)
    v = jnp.var(x, axis=axis, keepdims=True)
    return (x - m) / jnp.sqrt(v + eps)

def _scatter_add(tgt, idx, src, axis=0):
    return tgt.at[idx].add(src)

def _segment_sum(src, seg, n):
    return jax.ops.segment_sum(src, seg, n)
kernel_name = 'mk_adaln_d1_jaxref_r8_d82fc0'

def setup_inputs(seed: int=0):
    np.random.seed(seed)
    _w = jnp.asarray

    def _L0_attn_setup():
        import jax, jax.numpy as jnp
        import numpy as np
        B_SZ, L, D, N, H = (2, 256, 128, 16, 128)

        def celu(x):
            return jnp.where(x > 0, x, jnp.expm1(x))

        def _reference_tuple_inner(x, W1, b1, W2, b2, W3, b3, Wl1, bl1, Wl2, bl2, Wf1, bf1, Wf2, bf2, state_init, A):
            b = x.shape[0]
            lifted = jnp.tanh(jax.nn.relu(x @ Wl1 + bl1) @ Wl2 + bl2)
            combined = jnp.concatenate([x, lifted], axis=-1)
            x_trans = jax.nn.relu(combined @ Wf1 + bf1) @ Wf2 + bf2
            h_prev = jnp.broadcast_to(state_init, (b,) + state_init.shape[1:])
            Bm = x_trans @ W2 + b2
            Cm = x_trans @ W3 + b3
            delta = jax.nn.softplus(x_trans @ W1 + b1)
            dB = delta[..., :, None] * Bm[..., None, :]
            dA = jnp.exp(-celu(delta[..., :, None] * A[None, None]))
            h_new = dA * h_prev[:, None] + x_trans[..., None] * dB
            output = jnp.einsum('bln,bldn->bld', Cm, h_new)
            last_h_state = h_new[:, -1]
            return (output, last_h_state)
        key = jax.random.key(seed)
        ks = jax.random.split(key, 16)
        s = lambda fan_in: 1.0 / np.sqrt(fan_in)
        inp = {'x': jax.random.normal(ks[0], (B_SZ, L, D), jnp.float32), 'W1': jax.random.normal(ks[1], (D, D), jnp.float32) * s(D), 'b1': jnp.zeros((D,), jnp.float32), 'W2': jax.random.normal(ks[2], (D, N), jnp.float32) * s(D), 'b2': jnp.zeros((N,), jnp.float32), 'W3': jax.random.normal(ks[3], (D, N), jnp.float32) * s(D), 'b3': jnp.zeros((N,), jnp.float32), 'Wl1': jax.random.normal(ks[4], (D, H), jnp.float32) * s(D), 'bl1': jnp.zeros((H,), jnp.float32), 'Wl2': jax.random.normal(ks[5], (H, D), jnp.float32) * s(H), 'bl2': jnp.zeros((D,), jnp.float32), 'Wf1': jax.random.normal(ks[6], (2 * D, H), jnp.float32) * s(2 * D), 'bf1': jnp.zeros((H,), jnp.float32), 'Wf2': jax.random.normal(ks[7], (H, D), jnp.float32) * s(H), 'bf2': jnp.zeros((D,), jnp.float32), 'state_init': jnp.zeros((1, D, N), jnp.float32), 'A': jax.random.normal(ks[8], (D, N), jnp.float32) * np.sqrt(2.0 / N)}
        return inp
    _L0_attn_in = _L0_attn_setup()

    def _L0_ffn_setup():
        import jax, jax.numpy as jnp
        import numpy as np
        B, S, D, F, E = (4, 256, 128, 512, 8)
        key = jax.random.key(seed)
        ks = jax.random.split(key, 7)
        s1 = 1.0 / np.sqrt(D)
        s2 = 1.0 / np.sqrt(F)
        x = jax.random.normal(ks[0], (B, S, D), dtype=jnp.float32)
        W1 = jax.random.uniform(ks[1], (E, D, F), jnp.float32, -s1, s1)
        b1 = jax.random.uniform(ks[2], (E, F), jnp.float32, -s1, s1)
        W2 = jax.random.uniform(ks[3], (E, F, D), jnp.float32, -s2, s2)
        b2 = jax.random.uniform(ks[4], (E, D), jnp.float32, -s2, s2)
        Wr = jax.random.uniform(ks[5], (D, E), jnp.float32, -s1, s1)
        br = jax.random.uniform(ks[6], (E,), jnp.float32, -s1, s1)
        return {'x': x, 'W1': W1, 'b1': b1, 'W2': W2, 'b2': b2, 'Wr': Wr, 'br': br}
    _L0_ffn_in = _L0_ffn_setup()
    _L0_c = _w((lambda *s: np.random.randn(*s).astype(np.float32) * 0.05)(8, 128))
    _L0_wmod = _w((lambda *s: np.random.randn(*s).astype(np.float32) * 0.05)(128, 6 * 128) * 128 ** (-0.5))
    _d = {'L0_attn_x': _L0_attn_in['x'], 'L0_attn_W1': _L0_attn_in['W1'], 'L0_attn_b1': _L0_attn_in['b1'], 'L0_attn_W2': _L0_attn_in['W2'], 'L0_attn_b2': _L0_attn_in['b2'], 'L0_attn_W3': _L0_attn_in['W3'], 'L0_attn_b3': _L0_attn_in['b3'], 'L0_attn_Wl1': _L0_attn_in['Wl1'], 'L0_attn_bl1': _L0_attn_in['bl1'], 'L0_attn_Wl2': _L0_attn_in['Wl2'], 'L0_attn_bl2': _L0_attn_in['bl2'], 'L0_attn_Wf1': _L0_attn_in['Wf1'], 'L0_attn_bf1': _L0_attn_in['bf1'], 'L0_attn_Wf2': _L0_attn_in['Wf2'], 'L0_attn_bf2': _L0_attn_in['bf2'], 'L0_attn_state_init': _L0_attn_in['state_init'], 'L0_attn_A': _L0_attn_in['A'], 'L0_ffn_W1': _L0_ffn_in['W1'], 'L0_ffn_b1': _L0_ffn_in['b1'], 'L0_ffn_W2': _L0_ffn_in['W2'], 'L0_ffn_b2': _L0_ffn_in['b2'], 'L0_ffn_Wr': _L0_ffn_in['Wr'], 'L0_ffn_br': _L0_ffn_in['br'], 'L0_c': _L0_c, 'L0_wmod': _L0_wmod}
    _x0 = _d['L0_attn_x']
    _d['L0_attn_x'] = jax.random.normal(jax.random.fold_in(jax.random.key(seed), 1), (8, 1024, 128), dtype=_x0.dtype)
    del _x0
    return _d

def reference(L0_attn_x, L0_attn_W1, L0_attn_b1, L0_attn_W2, L0_attn_b2, L0_attn_W3, L0_attn_b3, L0_attn_Wl1, L0_attn_bl1, L0_attn_Wl2, L0_attn_bl2, L0_attn_Wf1, L0_attn_bf1, L0_attn_Wf2, L0_attn_bf2, L0_attn_state_init, L0_attn_A, L0_ffn_W1, L0_ffn_b1, L0_ffn_W2, L0_ffn_b2, L0_ffn_Wr, L0_ffn_br, L0_c, L0_wmod):

    def _L0_attn_ref(x, W1, b1, W2, b2, W3, b3, Wl1, bl1, Wl2, bl2, Wf1, bf1, Wf2, bf2, state_init, A):
        import jax, jax.numpy as jnp
        import numpy as np
        B_SZ, L, D, N, H = (2, 256, 128, 16, 128)

        def celu(x):
            return jnp.where(x > 0, x, jnp.expm1(x))

        def _reference_tuple_inner(x, W1, b1, W2, b2, W3, b3, Wl1, bl1, Wl2, bl2, Wf1, bf1, Wf2, bf2, state_init, A):
            b = x.shape[0]
            lifted = jnp.tanh(jax.nn.relu(x @ Wl1 + bl1) @ Wl2 + bl2)
            combined = jnp.concatenate([x, lifted], axis=-1)
            x_trans = jax.nn.relu(combined @ Wf1 + bf1) @ Wf2 + bf2
            h_prev = jnp.broadcast_to(state_init, (b,) + state_init.shape[1:])
            Bm = x_trans @ W2 + b2
            Cm = x_trans @ W3 + b3
            delta = jax.nn.softplus(x_trans @ W1 + b1)
            dB = delta[..., :, None] * Bm[..., None, :]
            dA = jnp.exp(-celu(delta[..., :, None] * A[None, None]))
            h_new = dA * h_prev[:, None] + x_trans[..., None] * dB
            output = jnp.einsum('bln,bldn->bld', Cm, h_new)
            last_h_state = h_new[:, -1]
            return (output, last_h_state)
        return _reference_tuple_inner(x, W1, b1, W2, b2, W3, b3, Wl1, bl1, Wl2, bl2, Wf1, bf1, Wf2, bf2, state_init, A)[0]

    def _L0_ffn_ref(x, W1, b1, W2, b2, Wr, br):
        import jax, jax.numpy as jnp
        import numpy as np
        B, S, D, F, E = (4, 256, 128, 512, 8)
        b, s, d = x.shape
        e = Wr.shape[1]
        logits = x @ Wr + br
        idx = jnp.argmax(logits, axis=-1)
        probs = jax.nn.softmax(logits, axis=-1)
        gates = jnp.take_along_axis(probs, idx[..., None], axis=-1)[..., 0]
        xf = x.reshape(-1, d)
        idxf = idx.reshape(-1)
        gf = gates.reshape(-1)
        out = jnp.zeros_like(xf)
        for ei in range(e):
            h = jax.nn.gelu(xf @ W1[ei] + b1[ei], approximate=False)
            y = h @ W2[ei] + b2[ei]
            mask = (idxf == ei).astype(xf.dtype)
            out = out + y * (gf * mask)[:, None]
        return out.reshape(b, s, d)
    x = L0_attn_x
    mod = (_silu(L0_c) @ L0_wmod).reshape(L0_c.shape[0], 6, 1, -1)
    sa, ca, ga, sb, cb, gb = (mod[:, 0], mod[:, 1], mod[:, 2], mod[:, 3], mod[:, 4], mod[:, 5])
    ga = (2 * (ga >= 0) - 1) * jnp.maximum(jnp.abs(ga), 0.25)
    gb = (2 * (gb >= 0) - 1) * jnp.maximum(jnp.abs(gb), 0.25)
    h = _layernorm(x, axis=-1) * (1 + ca) + sa
    x = x + ga * _L0_attn_ref(h, L0_attn_W1, L0_attn_b1, L0_attn_W2, L0_attn_b2, L0_attn_W3, L0_attn_b3, L0_attn_Wl1, L0_attn_bl1, L0_attn_Wl2, L0_attn_bl2, L0_attn_Wf1, L0_attn_bf1, L0_attn_Wf2, L0_attn_bf2, L0_attn_state_init, L0_attn_A)
    h = _layernorm(x, axis=-1) * (1 + cb) + sb
    x = x + gb * _L0_ffn_ref(h, L0_ffn_W1, L0_ffn_b1, L0_ffn_W2, L0_ffn_b2, L0_ffn_Wr, L0_ffn_br)
    return x

_drawn_inputs = setup_inputs


def setup_inputs(seed=0):
    import zlib

    import numpy as np

    out = dict(_drawn_inputs(seed))
    spreads = {'L0_attn_b1': (0.0, 0.756),
     'L0_attn_b2': (0.0, 0.335),
     'L0_attn_b3': (0.0, 0.364),
     'L0_attn_bl1': (0.0, 0.611),
     'L0_attn_bl2': (0.0, 0.478),
     'L0_attn_bf1': (0.0, 0.1),
     'L0_attn_bf2': (0.0, 0.1),
     'L0_attn_state_init': (0.0, 0.1)}
    factors = {'L0_attn_A': 3.581,
     'L0_ffn_W1': 4.682,
     'L0_ffn_b1': 8.0,
     'L0_ffn_W2': 4.41,
     'L0_ffn_b2': 8.0,
     'L0_ffn_Wr': 4.685,
     'L0_ffn_br': 8.0}
    for name, (base, spread) in spreads.items():
        noise = np.random.default_rng([zlib.crc32(name.encode()), seed]).standard_normal(out[name].shape)
        drawn = base * np.exp(spread * noise) if base else spread * noise
        out[name] = jnp.asarray(drawn.astype(out[name].dtype))
    for name, factor in factors.items():
        out[name] = (out[name] * factor).astype(out[name].dtype)
    return out
```

```python
from contextlib import ExitStack

import concourse.bass as bass
from concourse import mybir

ALU = mybir.AluOpType
ACT = mybir.ActivationFunctionType
AX = mybir.AxisListType
F32 = mybir.dt.float32
BF16 = mybir.dt.bfloat16
U32 = mybir.dt.uint32
I32 = mybir.dt.int32

P = 128
B, L, D = 8, 1024, 128
N = 16
E = 8
F = 512
FC = F // P
T = B * L
CH = 512
J = CH // P
NCH = T // CH
CPB = L // CH
assert CPB == 2
DG = P // N
NQ = 4
NK = D // DG // NQ
REGION = T + P
NT = T // P + E
DEAD = E * REGION
NO_TOKEN = 1 << 20
ROW = 3 * D + 1
EPS = 1e-5
TANH_CLAMP = 20.0
SOFTPLUS_CLAMP = 30.0
W1C = F + FC

C_ID = 0
C_TRI = C_ID + P
C_SEL = C_TRI + P
C_MASK = C_SEL + NK * P
C_PRI = C_MASK + NK * NQ * 32
C_BASE = C_PRI + J * E
C_TILE = C_BASE + E
C_STEP = C_TILE + NT
C_PART = C_STEP + T // P
C_TOK = C_PART + 1
C_ALL = C_TOK + J

MASKED = NK * NQ * 32

SLOTS = 16
TILE_SLOTS = 4
RING = 8


class Item:

    def __init__(self, n, q, ring, round):
        self.n, self.q, self.ring, self.round = n, q, ring, round

    def static(self):
        return isinstance(self.n, int)

    def has(self, k):
        return not self.static() or self.n >= k

    def at(self, k):
        q = self.q + k
        return Item(self.n + k, q % self.ring, self.ring, self.round + q // self.ring)


def pipeline(engine, steps_of, total, slots, ring, loop_from, rounds, turns, before=None):
    def turn(item):
        found = []
        for k in range(-4, 5):
            other = item.at(-k)
            if item.static() and not 0 <= other.n < total:
                continue
            found += [(slot - k * slots, order, step) for order, (slot, step) in enumerate(steps_of(other))
                      if k * slots <= slot < (k + 1) * slots]
        for _, _, step in sorted(found, key=lambda x: x[0]):
            step()

    def peeled(ns):
        for n in ns:
            turn(Item(n, n % ring, ring, n // ring))

    peeled(range(turns[0], loop_from))
    with engine.Fori(0, rounds) as i:
        if before:
            before(i)
        for k in range(ring):
            turn(Item(i * ring + (loop_from + k), (loop_from + k) % ring, ring, i + (loop_from + k) // ring))
    peeled(range(loop_from + rounds * ring, turns[1]))


def build(nc, a, out):
    with ExitStack() as ctx:
        def sb(name, shape, dt=F32):
            return ctx.enter_context(nc.sbuf_tensor(name, shape, dt))

        def ps(name):
            return ctx.enter_context(nc.psum_tensor(name, [P, CH], F32))

        def sem(name):
            return ctx.enter_context(nc.semaphore(name))

        rows = nc.dram_tensor("rows", [E * REGION + P, ROW], F32, kind="Internal").ap()

        consts = sb("consts", [P, C_ALL])
        ident = consts[:, C_ID:C_ID + P]
        tri = sb("tri", [P, P], BF16)
        ones_bf = sb("ones_bf", [P, P], BF16)
        eighth = sb("eighth", [P, P])
        sel = sb("sel", [96, NK, P], BF16)
        hsel = sb("hsel", [P, NQ * NK, 32])
        smalls = sb("smalls", [P, 2 * N + 7])
        a_r = smalls[:, 0:N]
        h0_r = smalls[:, N:2 * N]
        a_neg = sb("a_neg", [P, N])
        a_pos = sb("a_pos", [P, N])
        b2r = smalls[:, 2 * N:2 * N + 1]
        b3r = smalls[:, 2 * N + 1:2 * N + 2]
        b1 = smalls[:, 2 * N + 2:2 * N + 3]
        bl1 = smalls[:, 2 * N + 3:2 * N + 4]
        bl2 = smalls[:, 2 * N + 4:2 * N + 5]
        bf1 = smalls[:, 2 * N + 5:2 * N + 6]
        bf2 = smalls[:, 2 * N + 6:2 * N + 7]
        w1 = sb("w1", [P, D])
        wl1 = sb("wl1", [P, D])
        wl2 = sb("wl2", [P, D])
        wf1 = sb("wf1", [P, 2, D])
        wf2 = sb("wf2", [P, D])
        w23 = sb("w23", [P, 2, N])
        w2r = sb("w2r", [P, N, DG])
        w3r = sb("w3r", [P, N, DG])
        wr = sb("wr", [P, E])
        br = sb("br", [P, E])
        ffn1 = sb("ffn1", [P, E, W1C])
        ffn2 = sb("ffn2", [P, E, FC, D])
        ffb2 = sb("ffb2", [P, E, D])
        ct = sb("ct", [P, B])
        c_work = sb("c_work", [P, 3, B])
        sc = sb("sc", [P, B])
        wmod = sb("wmod", [P, 6, D])
        mod_t = sb("mod_t", [P, 3, B])
        mod_g = sb("mod_g", [P, 2, B])
        mod_r = sb("mod_r", [P, B, 3, D])

        x_in = sb("x_in", [P, NCH, J * D])
        stats = sb("stats", [P, J, 6])
        mv = sb("mv", [P, 6, J])
        ve = sb("ve", [P, J])
        lnv = sb("lnv", [P, J])
        r0 = sb("r0", [P, J])
        nw = sb("nw", [P, 3, J])
        xn = sb("xn", [P, J, D])
        h1t = sb("h1t", [P, CH])
        a1 = sb("a1", [P, CH])
        th = sb("th", [P, 2, CH])
        lift = sb("lift", [P, CH])
        a3 = sb("a3", [P, CH])
        xt = sb("xt", [P, CH])
        sp = sb("sp", [P, 2, CH])
        delta = sb("delta", [P, CH])
        crep = sb("crep", [P, 2, CH])
        cb = sb("cb", [P, CH])
        dx = sb("dx", [P, CH])
        y2 = sb("y2", [P, 2, CH])
        part = sb("part", [P, 3, CH], BF16)
        rest = sb("rest", [P, CH])
        stk = sb("stk", [96, 2, NQ, CH], BF16)
        u = sb("u", [P, NK, NQ, CH])
        o = sb("o", [P, CH])
        stats2 = sb("stats2", [P, J, 6])
        mv2 = sb("mv2", [P, 6, J])
        ve2 = sb("ve2", [P, J])
        lnv2 = sb("lnv2", [P, J])
        r02 = sb("r02", [P, J])
        nw2 = sb("nw2", [P, 3, J])
        xn2 = sb("xn2", [P, J, D])
        mod_c = sb("mod_c", [P, 2, 2, D])
        hm = sb("hm", [P, J, D])
        h2t = sb("h2t", [P, CH])
        row = sb("row", [P, 2, J, ROW])
        lg = sb("lg", [P, J, E])
        mx = sb("mx", [P, J])
        df = sb("df", [P, J, E])
        ex = sb("ex", [P, J, E])
        se = sb("se", [P, J])
        gate = sb("gate", [P, J])
        score = sb("score", [P, J, E])
        eq = sb("eq", [P, J, E])
        picked = sb("picked", [P, J, E])
        ms = sb("ms", [P, J])
        oh = sb("oh", [P, J, E])
        ohb = sb("ohb", [P, J, E], BF16)
        base = sb("base", [P, J + 1, E])
        pos = sb("pos", [P, J, E])
        slotf = sb("slotf", [P, J])
        slot = sb("slot", [P, 2, J], U32)
        tok = sb("tok", [P, J])
        pad = sb("pad", [P, ROW])
        pad_at = sb("pad_at", [P, E + 1], U32)
        cnt = sb("cnt", [P, E])
        ntl = sb("ntl", [P, E])
        cum = sb("cum", [P, E])
        tile_e = sb("tile_e", [P, NT])
        tile_w = sb("tile_w", [P, 4, NT])
        tile_expert = sb("tile_expert", [P, NT], I32)
        tile_expert_3 = sb("tile_expert_3", [P, NT + 3], I32)
        tile_start = sb("tile_start", [P, NT + 3], I32)
        room = u[:, :, :, :].rearrange("p k q c -> p (k q c)")
        taken = [0]

        def in_u(*shape):
            n = 1
            for x in shape:
                n *= x
            v = room[:, taken[0]:taken[0] + n]
            taken[0] += n
            names = "abc"[:len(shape)]
            return v.rearrange(f"p ({' '.join(names)}) -> p {' '.join(names)}", **dict(zip(names, shape)))
        sc_rep = in_u(B, P)
        g_work = in_u(2, B * D)
        taken[0] = 0
        cmp = in_u(E, T // P)
        cmp2 = in_u(NT, E)
        cmp3 = in_u(NT, E)
        taken[0] = 0
        xs = in_u(RING, ROW)
        xst = in_u(2, P)
        w1s = in_u(2, W1C)
        hid = in_u(2, FC, P)
        ys = in_u(RING, 2, D)
        ids = sb("ids", [P, RING], U32)

        ps_0 = ps("ps_0")
        ps_1 = ps("ps_1")
        ps_2 = ps("ps_2")
        ps_d = [ps("ps_d0"), ps("ps_d1"), ps("ps_d2")]
        ps_o = ps("ps_o")
        ps_x = ps("ps_x")

        w_in = sem("w_in")
        ffn_in = sem("ffn_in")
        setup_v = sem("setup_v")
        setup_a = sem("setup_a")
        setup_p = sem("setup_p")
        setup_g = sem("setup_g")
        setup_chain = sem("setup_chain")
        x_here = [sem("x_here0"), sem("x_here1"), sem("x_here2")]
        v_norm = sem("v_norm")
        var_ready = sem("var_ready")
        var_log = sem("var_log")
        tanh_exp = sem("tanh_exp")
        tanh_log = sem("tanh_log")
        sp_exp = sem("sp_exp")
        rstd_ready = sem("rstd_ready")
        rstd_done = sem("rstd_done")
        xn_ready = sem("xn_ready")
        xn_turned = sem("xn_turned")
        h1_ready = sem("h1_ready")
        z1_ready = sem("z1_ready")
        a1_ready = sem("a1_ready")
        z2_ready = sem("z2_ready")
        tanh_arg = sem("tanh_arg")
        tanh_ready = sem("tanh_ready")
        lift_ready = sem("lift_ready")
        z3_ready = sem("z3_ready")
        a3_ready = sem("a3_ready")
        z4_ready = sem("z4_ready")
        xt_ready = sem("xt_ready")
        z5_ready = sem("z5_ready")
        zc_ready = sem("zc_ready")
        zb_ready = sem("zb_ready")
        sp_arg = sem("sp_arg")
        sp_log = sem("sp_log")
        delta_ready = sem("delta_ready")
        v_split = sem("v_split")
        c_ready = sem("c_ready")
        cb_ready = sem("cb_ready")
        s_ready = sem("s_ready")
        y2_ready = sem("y2_ready")
        parts_ready = sem("parts_ready")
        stk_here = [sem("stk_here0"), sem("stk_here1")]
        rep_ready = sem("rep_ready")
        e_ready = sem("e_ready")
        arg_ready = sem("arg_ready")
        g_ready = sem("g_ready")
        w_pool = sem("w_pool")
        w_dve = sem("w_dve")
        n_summed = sem("n_summed")
        o_ready = sem("o_ready")
        o_turned = sem("o_turned")
        x1_ready = sem("x1_ready")
        v_norm2 = sem("v_norm2")
        var2_ready = sem("var2_ready")
        var2_log = sem("var2_log")
        rstd2_ready = sem("rstd2_ready")
        rstd2_done = sem("rstd2_done")
        xn2_ready = sem("xn2_ready")
        pool_own = sem("pool_own")
        h2_ready = sem("h2_ready")
        h2_turned = sem("h2_turned")
        h2t_ready = sem("h2t_ready")
        logits_ready = sem("logits_ready")
        v_route = sem("v_route")
        logits_read = sem("logits_read")
        diff_ready = sem("diff_ready")
        ex_ready = sem("ex_ready")
        oh_ready = sem("oh_ready")
        counts_ready = sem("counts_ready")
        v_place = sem("v_place")
        ranks_read = sem("ranks_read")
        tok_next = sem("tok_next")
        row_ready = sem("row_ready")
        sent = [sem("sent0"), sem("sent1")]
        pad_ready = sem("pad_ready")
        pad_sent = sem("pad_sent")
        table_ready = sem("table_ready")
        xs_here = [sem(f"xs_here{i}") for i in range(RING)]
        xs_turned = sem("xs_turned")
        xst_ready = sem("xst_ready")
        w1s_ready = sem("w1s_ready")
        hid_psum = sem("hid_psum")
        hid_ready = sem("hid_ready")
        y_psum = sem("y_psum")
        v_y = sem("v_y")
        y_ready = sem("y_ready")
        stored = [sem(f"stored{i}") for i in range(RING)]

        NG = NK * NQ
        POOL_K = (0, 1, 2)
        DVE_K = (3,)
        CHUNKS = dict(total=NCH, slots=SLOTS, ring=2, loop_from=3, rounds=5, turns=(-3, NCH + 4))
        TILES = dict(total=NT, slots=TILE_SLOTS, ring=RING, loop_from=6, rounds=(NT - 9) // RING,
                     turns=(-4, NT + 4))
        assert 3 + 5 * 2 <= NCH - 3

        block = ctx.enter_context(nc.Block())

        N_W = 13

        def load_eight(e, table, at, limit):
            _, values = nc.values_load_multi_w_load_instructions(
                table[0:1, bass.ds(at, RING)], engines=[e.engine], min_val=0, max_val=limit)
            return values

        def picker(e, table, shift, ahead, limit):
            now = []

            def before(i):
                now[:] = load_eight(e, table, i * RING + (TILES["loop_from"] + ahead + shift), limit)

            def pick(t):
                if t.static():
                    return e.value_load(table[0:1, t.n + shift:t.n + shift + 1], min_val=0, max_val=limit)
                return now[(t.q - TILES["loop_from"] - ahead) % RING]
            return before, pick

        def mod_col(s, c):
            return mod_t[:, s, bass.ds(c.round, 1)]

        def bank(i):
            return i % 3 if i < NG - 1 else 1

        @block.sync
        def _(e):
            def load(dst, src):
                e.dma_start(dst, src).then_inc(w_in, 16)
            e.dma_start(x_in[:, 0, :], a["x"][0]).then_inc(x_here[0], 16)
            load(smalls[:, :], a["smalls"])
            load(ct[:, :], a["cT"])
            load(wmod[:, :, :], a["wmod"].rearrange("p (s d) -> p s d", s=6))
            load(consts[:, :], a["consts"])
            load(wl1[:, :], a["Wl1"])
            load(wl2[:, :], a["Wl2"])
            load(wf1[:, :, :], a["Wf1"].rearrange("(c p) h -> p c h", p=P))
            load(wf2[:, :], a["Wf2"])
            load(w1[:, :], a["W1"])
            load(w23[:, 0, :], a["W2"])
            load(w23[:, 1, :], a["W3"])
            load(wr[:, :], a["Wr"])
            load(br[:, :], a["br"].rearrange("(o e) -> o e", o=1).to_broadcast([P, E]))
            e.dma_start(x_in[:, 1, :], a["x"][1]).then_inc(x_here[1], 16)
            e.dma_start(x_in[:, 2:NCH, :], a["x"][2:NCH].rearrange("c p t -> p c t")).then_inc(x_here[2], 16)
            e.dma_start(ffn2[:, :, :, :], a["ffn_W2"]).then_inc(ffn_in, 16)
            e.dma_start(ffn1[:, :, 0:F], a["ffn_W1"]).then_inc(ffn_in, 16)
            e.dma_start(ffn1[:, :, F:W1C], a["ffn_b1"]).then_inc(ffn_in, 16)
            e.dma_start(ffb2[:, :, :].rearrange("p e d -> p (e d)"),
                        a["ffn_b2"].rearrange("(o e) d -> o (e d)", o=1).to_broadcast([P, E * D]))\
                .then_inc(ffn_in, 16)

            def stack(c):
                e.wait_ge(parts_ready, c.n + 1)
                if c.has(2):
                    e.wait_ge(rep_ready, (c.n - 1) * NG)
                for k in range(3):
                    for qd in range(NQ):
                        e.dma_start(stk[32 * k:32 * k + 32, c.q, qd, :], part[32 * qd:32 * qd + 32, k, :])\
                            .then_inc(stk_here[c.q], 16)
            pipeline(e, lambda c: [(-2, lambda: stack(c))], **CHUNKS)

            e.wait_ge(table_ready, 1)
            e.wait_ge(sent[0], 16 * J * NCH // 2)
            e.wait_ge(sent[1], 16 * J * NCH // 2)
            e.wait_ge(pad_sent, 16 * (E + 1))
            before, start_of = picker(e, tile_start, 3, 3, DEAD)

            def tile_load(t):
                start = start_of(t)
                if t.has(RING):
                    e.wait_ge(y_ready, t.n - RING + 1)
                e.dma_start(xs[:, t.q, :], rows[bass.ds(start, P), :]).then_inc(xs_here[t.q], 16)
            pipeline(e, lambda t: [(-12, lambda: tile_load(t))], before=before, **TILES)

        @block.scalar
        def _(e):
            e.preload_act_table_set("natural_log_exp_and_others")
            e.wait_ge(w_in, 16 * N_W)
            e.activation(c_work[:, 0, :], ct[:, :], ACT.Exp, scale=-1.0).then_inc(setup_a, 1)
            e.wait_ge(setup_v, 3)

            def chunk_steps(c):
                def ln_var():
                    e.wait_ge(var_ready, c.n + 1)
                    e.activation(lnv[:, :], ve[:, :], ACT.Ln).then_inc(var_log, 1)

                def rstd():
                    e.wait_ge(var_log, c.n + 1)
                    e.activation(r0[:, :], lnv[:, :], ACT.Exp, scale=-0.5).then_inc(rstd_ready, 1)

                def h1():
                    e.wait_ge(xn_turned, c.n + 1)
                    e.wait_ge(z3_ready, c.n)
                    e.activation(h1t[:, :], ps_2[:, :], ACT.Identity, bias=mod_col(0, c), scale=mod_col(1, c))\
                        .then_inc(h1_ready, 1)

                def a1_():
                    e.wait_ge(z1_ready, c.n + 1)
                    e.activation(a1[:, :], ps_0[:, :], ACT.Relu, bias=bl1).then_inc(a1_ready, 1)

                def tanh_1():
                    e.wait_ge(tanh_arg, c.n + 1)
                    e.activation(th[:, 1, :], th[:, 0, :], ACT.Exp, scale=2.0).then_inc(tanh_exp, 1)

                def tanh_2():
                    e.wait_ge(tanh_exp, c.n + 1)
                    e.activation(th[:, 0, :], th[:, 1, :], ACT.Ln, bias=1.0).then_inc(tanh_log, 1)

                def tanh_3():
                    e.wait_ge(tanh_log, c.n + 1)
                    e.activation(th[:, 1, :], th[:, 0, :], ACT.Exp, scale=-1.0).then_inc(tanh_ready, 1)

                def x_trans():
                    e.wait_ge(z4_ready, c.n + 1)
                    e.wait_ge(zb_ready, c.n)
                    e.wait_ge(y2_ready, c.n)
                    e.activation(xt[:, :], ps_0[:, :], ACT.Identity, bias=bf2).then_inc(xt_ready, 1)

                def c_rep():
                    e.wait_ge(zc_ready, c.n + 1)
                    if c.has(2):
                        e.wait_ge(n_summed, NK * (c.n - 1))
                    e.activation(crep[:, c.q, :], ps_0[:, :], ACT.Identity, bias=b3r).then_inc(c_ready, 1)

                def softplus_1():
                    e.wait_ge(sp_arg, c.n + 1)
                    e.activation(sp[:, 1, :], sp[:, 0, :], ACT.Exp).then_inc(sp_exp, 1)

                def softplus_2():
                    e.wait_ge(sp_exp, c.n + 1)
                    e.activation(sp[:, 0, :], sp[:, 1, :], ACT.Ln, bias=1.0).then_inc(sp_log, 1)

                def exp_1(i):
                    k, qd = i // NQ, i % NQ
                    e.wait_ge(rep_ready, NG * c.n + i + 1)
                    if qd == 0 and c.has(1):
                        e.wait_ge(n_summed, NK * (c.n - 1) + k + 1)
                    e.activation(u[:, k, qd, :], ps_d[bank(i)][:, :], ACT.Exp,
                                 scale=a_neg[:, NK * qd + k:NK * qd + k + 1]).then_inc(e_ready, 1)

                def exp_2(k):
                    e.wait_ge(arg_ready, NG * c.n + NQ * (k + 1))
                    e.activation(u[:, k, :, :], u[:, k, :, :], ACT.Exp, scale=-1.0, bias=1.0).then_inc(g_ready, 1)

                def ln_var2():
                    e.wait_ge(var2_ready, c.n + 1)
                    e.activation(lnv2[:, :], ve2[:, :], ACT.Ln).then_inc(var2_log, 1)

                def rstd2():
                    e.wait_ge(var2_log, c.n + 1)
                    e.activation(r02[:, :], lnv2[:, :], ACT.Exp, scale=-0.5).then_inc(rstd2_ready, 1)

                def h2():
                    e.wait_ge(h2_turned, c.n + 1)
                    e.wait_ge(logits_ready, c.n)
                    e.activation(h2t[:, :], ps_x[:, :], ACT.Copy).then_inc(h2t_ready, 1)

                def probs():
                    e.wait_ge(diff_ready, c.n + 1)
                    e.activation(ex[:, :, :], df[:, :, :], ACT.Exp).then_inc(ex_ready, 1)
                return ([(i + 1, lambda i=i: exp_1(i)) for i in range(NG)]
                        + [(NQ * k + 6, lambda k=k: exp_2(k)) for k in range(NK)]
                        + [(-32, ln_var), (-31, rstd), (-24, h1), (-22, a1_), (-19, tanh_1), (-18, tanh_2),
                           (-17, tanh_3), (-12, x_trans), (-9, softplus_1), (-9, c_rep), (-8, softplus_2),
                           (31, ln_var2), (32, rstd2), (40, h2), (46, probs)])
            pipeline(e, chunk_steps, **CHUNKS)

            def gelu(t):
                e.wait_ge(hid_psum, t.n + 1)
                if t.has(2):
                    e.wait_ge(y_psum, t.n - 1)
                for f in range(FC):
                    ins = e.activation(hid[:, t.q % 2, f, :], (ps_0, ps_1)[t.q % 2][:, f * P:(f + 1) * P], ACT.Gelu,
                                       bias=w1s[:, t.q % 2, F + f:F + f + 1])
                ins.then_inc(hid_ready, 1)
            pipeline(e, lambda t: [(2, lambda: gelu(t))], **TILES)

        @block.tensor
        def _(e):
            e.wait_ge(setup_v, 1)
            for s in range(3):
                ins = e.matmul(ps_2[:, s * B:(s + 1) * B], wmod[:, s, :], sc[:, :], start=True, stop=True)
            ins.then_inc(setup_p, 1)
            for b in range(B):
                if b >= 2:
                    e.wait_ge(setup_g, b - 1)
                e.matmul((ps_0, ps_1)[b % 2][:, 0:3 * D], sc_rep[:, b, :], wmod[:, 3:6, :], start=True, stop=True)\
                    .then_inc(setup_p, 1)
            e.wait_ge(setup_g, B)
            e.wait_ge(setup_v, 3)

            def chunk_steps(c):
                def turn():
                    e.wait_ge(xn_ready, c.n + 1)
                    if c.has(2):
                        e.wait_ge(y2_ready, c.n - 1)
                    for j in range(J):
                        ins = e.transpose(ps_2[:, j * P:(j + 1) * P], xn[:, j, :], ident)
                    ins.then_inc(xn_turned, 1)

                def z1():
                    e.wait_ge(h1_ready, c.n + 1)
                    e.wait_ge(c_ready, c.n)
                    e.matmul(ps_0[:, :], wl1[:, :], h1t[:, :], start=True, stop=True).then_inc(z1_ready, 1)

                def z2():
                    e.wait_ge(a1_ready, c.n + 1)
                    e.matmul(ps_0[:, :], wl2[:, :], a1[:, :], start=True, stop=True).then_inc(z2_ready, 1)

                def z3():
                    e.wait_ge(lift_ready, c.n + 1)
                    e.wait_ge(delta_ready, c.n)
                    if c.has(4):
                        e.wait_ge(logits_read, c.n - 3)
                    e.matmul(ps_1[:, :], wf1[:, 0, :], h1t[:, :], start=True, stop=False)
                    e.matmul(ps_1[:, :], wf1[:, 1, :], lift[:, :], start=False, stop=True).then_inc(z3_ready, 1)

                def z4():
                    e.wait_ge(a3_ready, c.n + 1)
                    e.matmul(ps_0[:, :], wf2[:, :], a3[:, :], start=True, stop=True).then_inc(z4_ready, 1)

                def z5():
                    e.wait_ge(xt_ready, c.n + 1)
                    e.matmul(ps_1[:, :], w1[:, :], xt[:, :], start=True, stop=True).then_inc(z5_ready, 1)
                    e.matmul(ps_0[:, :], w3r[:, :, :].rearrange("p n d -> p (n d)"), xt[:, :],
                             start=True, stop=True).then_inc(zc_ready, 1)

                def zb():
                    if not c.static() or c.n + 1 < NCH:
                        e.wait_ge(h1_ready, c.n + 2)
                    e.matmul(ps_2[:, :], w2r[:, :, :].rearrange("p n d -> p (n d)"), xt[:, :],
                             start=True, stop=True).then_inc(zb_ready, 1)

                def s():
                    e.wait_ge(cb_ready, c.n + 1)
                    e.matmul(ps_2[:, :], eighth[:, :], cb[:, :], start=True, stop=True).then_inc(s_ready, 1)

                def rep(i):
                    if i == 0:
                        e.wait_ge(stk_here[c.q], (c.round + 1) * 16 * 3 * NQ)
                    last = max(g for g in range(-NG, i) if bank(g % NG) == bank(i))
                    if last >= 0 or c.has(1):
                        e.wait_ge(arg_ready, NG * c.n + last + 1)
                    e.matmul(ps_d[bank(i)][:, :], sel[:, i // NQ, :], stk[:, c.q, i % NQ, :], start=True, stop=True)\
                        .then_inc(rep_ready, 1)

                def summed(k):
                    if k in POOL_K:
                        e.wait_ge(w_pool, len(POOL_K) * c.n + POOL_K.index(k) + 1)
                    else:
                        e.wait_ge(w_dve, len(DVE_K) * c.n + DVE_K.index(k) + 1)
                    if k == 0:
                        e.wait_ge(o_ready, c.n)
                    for qd in range(NQ):
                        ins = e.matmul(ps_o[32 * qd:32 * qd + 32, :], hsel[:, NK * qd + k, :], u[:, k, qd, :],
                                       start=(k == 0), stop=(k == NK - 1))
                    ins.then_inc(n_summed, 1)

                def turn_o():
                    e.wait_ge(o_ready, c.n + 1)
                    if c.has(1):
                        e.wait_ge(h2t_ready, c.n)
                    for j in range(J):
                        ins = e.transpose(ps_x[:, j * P:(j + 1) * P], o[:, j * P:(j + 1) * P], ident)
                    ins.then_inc(o_turned, 1)

                def turn_h2():
                    e.wait_ge(h2_ready, c.n + 1)
                    e.wait_ge(x1_ready, c.n + 1)
                    if c.has(1):
                        e.wait_ge(ranks_read, c.n)
                    for j in range(J):
                        ins = e.transpose(ps_x[:, j * P:(j + 1) * P], row[:, c.q, j, 0:D], ident)
                    ins.then_inc(h2_turned, 1)

                def logits():
                    e.wait_ge(h2t_ready, c.n + 1)
                    e.wait_ge(delta_ready, min(c.n + 4, NCH) if c.static() else c.n + 4)
                    for j in range(J):
                        ins = e.matmul(ps_1[:, j * E:(j + 1) * E], h2t[:, j * P:(j + 1) * P], wr[:, :],
                                       start=True, stop=True)
                    ins.then_inc(logits_ready, 1)

                def ranks():
                    e.wait_ge(oh_ready, c.n + 1)
                    e.wait_ge(x1_ready, min(c.n + 2, NCH) if c.static() else c.n + 2)
                    v = ohb[:, :, :].rearrange("p j e -> p (j e)")
                    e.matmul(ps_x[:, 0:J * E], tri[:, :], v, start=True, stop=True)
                    e.matmul(ps_x[:, 64:64 + J * E], ones_bf[:, :], v, start=True, stop=True)\
                        .then_inc(counts_ready, 1)
                return ([(i, lambda i=i: rep(i)) for i in range(NG)]
                        + [((12, 16, 20, 22)[k], lambda k=k: summed(k)) for k in range(NK)]
                        + [(-25, turn), (-23, z1), (-21, z2), (-15, z3), (-13, z4), (-11, z5), (-7, zb), (-3, s),
                           (25, turn_o), (39, turn_h2), (42, logits), (50, ranks)])
            pipeline(e, chunk_steps, **CHUNKS)

            e.wait_ge(table_ready, 1)
            e.wait_ge(ffn_in, 64)
            before, expert_of = picker(e, tile_expert_3, 3, -1, E - 1)

            def tile_steps(t):
                def turn():
                    e.wait_ge(xs_here[t.q], 16 * (t.round + 1))
                    if t.has(2):
                        e.wait_ge(xst_ready, t.n - 1)
                    e.transpose(ps_d[t.q % 2][:, 0:P], xs[:, t.q, 0:D], ident).then_inc(xs_turned, 1)

                def first():
                    e.wait_ge(xst_ready, t.n + 1)
                    e.wait_ge(w1s_ready, t.n + 1)
                    if t.has(2):
                        e.wait_ge(hid_ready, t.n - 1)
                    for f in range(FC):
                        ins = e.matmul((ps_0, ps_1)[t.q % 2][:, f * P:(f + 1) * P],
                                       w1s[:, t.q % 2, f * P:(f + 1) * P], xst[:, t.q % 2, :], start=True, stop=True)
                    ins.then_inc(hid_psum, 1)

                def second():
                    x = expert_of(t)
                    e.wait_ge(hid_ready, t.n + 1)
                    if t.has(2):
                        e.wait_ge(v_y, 2 * t.n - 3)
                    for f in range(FC):
                        ins = e.matmul((ps_o, ps_x)[t.q % 2][:, 0:D], hid[:, t.q % 2, f, :],
                                       ffn2[:, bass.ds(x, 1), f, :].rearrange("p o d -> p (o d)"),
                                       start=(f == 0), stop=(f == FC - 1))
                    ins.then_inc(y_psum, 1)
                return [(-4, turn), (0, first), (5, second)]
            pipeline(e, tile_steps, before=before, **TILES)

        @block.vector
        def _(e):
            steps = [0]

            def then(ins):
                steps[0] += 1
                ins.then_inc(setup_chain, 1)
                e.wait_ge(setup_chain, steps[0])

            e.wait_ge(w_in, 16 * N_W)
            e.wait_ge(setup_a, 1)
            then(e.tensor_scalar(c_work[:, 1, :], c_work[:, 0, :], 1.0, None, ALU.add))
            then(e.reciprocal(c_work[:, 2, :], c_work[:, 1, :]))
            then(e.tensor_tensor(sc[:, :], ct[:, :], c_work[:, 2, :], ALU.mult))
            e.tensor_copy(sc_rep[:, :, :], sc[:, :].unsqueeze(2).broadcast_to([P, B, P])).then_inc(setup_v, 1)
            e.memset(ones_bf[:, :], 1.0)
            e.memset(eighth[:, :], 1.0 / DG)
            e.tensor_copy(tri[:, :], consts[:, C_TRI:C_TRI + P])
            e.tensor_copy(sel[:, :, :].rearrange("p k m -> p (k m)"), consts[0:96, C_SEL:C_SEL + NK * P])
            e.tensor_tensor(hsel[:, :, :], consts[:, C_MASK:C_MASK + MASKED].rearrange("p (g m) -> p g m", m=32),
                            h0_r.unsqueeze(2).broadcast_to([P, NQ * NK, 32]), ALU.mult)
            e.tensor_scalar(a_neg[:, :], a_r, 0.0, None, ALU.min)
            e.tensor_scalar(a_pos[:, :], a_r, 0.0, None, ALU.max)
            e.tensor_copy(w2r[:, :, :], w23[:, 0, :].unsqueeze(2).broadcast_to([P, N, DG]))
            e.tensor_copy(w3r[:, :, :], w23[:, 1, :].unsqueeze(2).broadcast_to([P, N, DG]))
            e.tensor_copy(tok[:, :], consts[:, C_TOK:C_TOK + J])
            e.tensor_copy(base[:, J, :], consts[:, C_BASE:C_BASE + E])
            e.memset(pad[:, 0:ROW - 1], 0.0)
            e.wait_ge(setup_p, 1)
            then(e.tensor_copy(mod_t[:, :, :], ps_2[:, 0:3 * B].rearrange("p (s b) -> p s b", b=B)))
            then(e.tensor_scalar(mod_t[:, 1, :], mod_t[:, 1, :], 1.0, None, ALU.add))

            def clamped(g, work):
                absolute, sign = work
                then(e.scalar_tensor_tensor(out=absolute, in0=g, scalar=-1.0, in1=g, op0=ALU.mult, op1=ALU.max))
                then(e.tensor_scalar(absolute, absolute, 0.25, None, ALU.max))
                then(e.tensor_scalar(sign, g, 0.0, 2.0, ALU.is_ge, ALU.mult))
                then(e.tensor_scalar(sign, sign, -1.0, None, ALU.add))
                then(e.tensor_tensor(g, sign, absolute, ALU.mult))
            clamped(mod_t[:, 2, :], (mod_g[:, 0, :], mod_g[:, 1, :]))
            for b in range(B):
                e.wait_ge(setup_p, b + 2)
                e.tensor_copy(mod_r[:, b, :, :].rearrange("p s d -> p (s d)"), (ps_0, ps_1)[b % 2][:, 0:3 * D])\
                    .then_inc(setup_g, 1)
            e.wait_ge(setup_g, B)
            then(e.tensor_scalar(mod_r[:, :, 1, :], mod_r[:, :, 1, :], 1.0, None, ALU.add))
            clamped(mod_r[:, :, 2, :], tuple(g_work[:, i, :].rearrange("p (b d) -> p b d", b=B) for i in range(2)))
            e.memset(pad[:, ROW - 1:ROW].bitcast(U32), NO_TOKEN).then_inc(setup_v, 2)

            def norm_steps(c, src, st, m, v, w, own, ready, rstd, first, dst, before, after, slots):
                def stats_():
                    before()
                    for j in range(J):
                        ins = e.bn_stats(st[:, j, :], src(j))
                    ins.then_inc(own, 1)

                def sums():
                    e.wait_ge(own, 5 * c.n + 1)
                    e.tensor_tensor(m[:, 0, :], st[:, :, 1], st[:, :, 4], ALU.add)
                    e.tensor_tensor(m[:, 1, :], st[:, :, 1], st[:, :, 4], ALU.subtract)
                    e.tensor_tensor(m[:, 2, :], st[:, :, 2], st[:, :, 5], ALU.add).then_inc(own, 1)

                def moments():
                    e.wait_ge(own, 5 * c.n + 2)
                    e.tensor_tensor(m[:, 3, :], m[:, 1, :], m[:, 1, :], ALU.mult)
                    e.tensor_scalar(m[:, 4, :], m[:, 2, :], 1.0 / D, EPS, ALU.mult, ALU.add)
                    e.tensor_scalar(m[:, 5, :], m[:, 0, :], 0.5, None, ALU.mult).then_inc(own, 1)

                def variance():
                    e.wait_ge(own, 5 * c.n + 3)
                    e.scalar_tensor_tensor(out=v[:, :], in0=m[:, 3, :], scalar=0.25, in1=m[:, 4, :],
                                           op0=ALU.mult, op1=ALU.add).then_inc(ready, 1)

                def newton_1():
                    e.wait_ge(rstd, c.n + 1)
                    e.tensor_tensor(w[:, 0, :], first[:, :], first[:, :], ALU.mult).then_inc(own, 1)

                def newton_2():
                    e.wait_ge(own, 5 * c.n + 4)
                    e.scalar_tensor_tensor(out=w[:, 1, :], in0=w[:, 0, :], scalar=-0.5, in1=v[:, :],
                                           op0=ALU.mult, op1=ALU.mult).then_inc(own, 1)

                def newton_3():
                    e.wait_ge(own, 5 * c.n + 5)
                    e.scalar_tensor_tensor(out=w[:, 2, :], in0=w[:, 1, :], scalar=1.5, in1=first[:, :],
                                           op0=ALU.add, op1=ALU.mult).then_inc(after[0], 1)

                def apply():
                    e.wait_ge(after[0], c.n + 1)
                    after[1]()
                    for j in range(J):
                        ins = e.tensor_scalar(dst[:, j, :], src(j), m[:, 5, j:j + 1], w[:, 2, j:j + 1],
                                              ALU.subtract, ALU.mult)
                    ins.then_inc(after[2], 1)
                return list(zip(slots, (stats_, sums, moments, variance, newton_1, newton_2, newton_3, apply)))

            def chunk_steps(c):
                def x_of(j):
                    if c.static():
                        return x_in[:, c.n, j * D:(j + 1) * D]
                    return x_in[:, bass.ds(c.n, 1), j * D:(j + 1) * D].rearrange("p o d -> p (o d)")

                norm1 = norm_steps(
                    c, x_of, stats, mv, ve, nw, v_norm, var_ready, rstd_ready, r0, xn,
                    before=lambda: e.wait_ge(x_here[min(c.n, 2) if c.static() else 2], 16),
                    after=(rstd_done, lambda: e.wait_ge(xn_turned, c.n), xn_ready),
                    slots=(-36, -35, -34, -33, -30, -29, -28, -27))

                def tanh_in():
                    e.wait_ge(z2_ready, c.n + 1)
                    e.tensor_scalar(th[:, 0, :], ps_0[:, :], bl2, TANH_CLAMP, ALU.add, ALU.min)\
                        .then_inc(tanh_arg, 1)

                def lifted():
                    e.wait_ge(tanh_ready, c.n + 1)
                    e.wait_ge(z3_ready, c.n)
                    e.tensor_scalar(lift[:, :], th[:, 1, :], -2.0, 1.0, ALU.mult, ALU.add).then_inc(lift_ready, 1)

                def relu3():
                    e.wait_ge(z3_ready, c.n + 1)
                    e.wait_ge(z4_ready, c.n)
                    e.tensor_scalar(a3[:, :], ps_1[:, :], bf1, 0.0, ALU.add, ALU.max).then_inc(a3_ready, 1)

                def softplus_in():
                    e.wait_ge(z5_ready, c.n + 1)
                    e.tensor_scalar(sp[:, 0, :], ps_1[:, :], b1, SOFTPLUS_CLAMP, ALU.add, ALU.min)\
                        .then_inc(sp_arg, 1)

                def softplus_out():
                    e.wait_ge(sp_log, c.n + 1)
                    e.scalar_tensor_tensor(out=delta[:, :], in0=ps_1[:, :], scalar=b1, in1=sp[:, 0, :],
                                           op0=ALU.add, op1=ALU.max).then_inc(delta_ready, 1)

                def split_1():
                    e.wait_ge(delta_ready, c.n + 1)
                    if c.q == 1:
                        e.wait_ge(stk_here[0], 16 * 3 * NQ * (c.round + 1))
                    elif c.has(1):
                        e.wait_ge(stk_here[1], 16 * 3 * NQ * c.round)
                    e.tensor_copy(part[:, 0, :], delta[:, :]).then_inc(v_split, 1)

                def split_2():
                    e.wait_ge(v_split, 4 * c.n + 1)
                    e.tensor_tensor(rest[:, :], delta[:, :], part[:, 0, :], ALU.subtract).then_inc(v_split, 1)

                def split_3():
                    e.wait_ge(v_split, 4 * c.n + 2)
                    e.tensor_copy(part[:, 1, :], rest[:, :]).then_inc(v_split, 1)

                def split_4():
                    e.wait_ge(v_split, 4 * c.n + 3)
                    e.tensor_tensor(part[:, 2, :], rest[:, :], part[:, 1, :], ALU.subtract)\
                        .then_inc(parts_ready, 1)

                def cb_():
                    e.wait_ge(zb_ready, c.n + 1)
                    e.wait_ge(c_ready, c.n + 1)
                    e.wait_ge(s_ready, c.n)
                    e.scalar_tensor_tensor(out=cb[:, :], in0=ps_2[:, :], scalar=b2r, in1=crep[:, c.q, :],
                                           op0=ALU.add, op1=ALU.mult).then_inc(cb_ready, 1)

                def dx_():
                    e.tensor_tensor(dx[:, :], delta[:, :], xt[:, :], ALU.mult).then_inc(v_split, 1)

                def second_term():
                    e.wait_ge(v_split, 4 * c.n + 4)
                    e.wait_ge(s_ready, c.n + 1)
                    e.scalar_tensor_tensor(out=y2[:, c.q, :], in0=ps_2[:, :], scalar=mod_col(2, c), in1=dx[:, :],
                                           op0=ALU.mult, op1=ALU.mult).then_inc(y2_ready, 1)

                def arg(i):
                    k, qd = i // NQ, i % NQ
                    g = NK * qd + k
                    e.wait_ge(e_ready, NG * c.n + i + 1)
                    e.scalar_tensor_tensor(out=u[:, k, qd, :], in0=ps_d[bank(i)][:, :], scalar=a_pos[:, g:g + 1],
                                           in1=u[:, k, qd, :], op0=ALU.mult, op1=ALU.add).then_inc(arg_ready, 1)

                def weighed(k):
                    e.wait_ge(g_ready, NK * c.n + k + 1)
                    e.tensor_tensor(u[:, k, :, :], u[:, k, :, :],
                                    crep[:, c.q, :].unsqueeze(1).broadcast_to([P, NQ, CH]), ALU.mult)\
                        .then_inc(w_dve, 1)

                def first_term():
                    e.wait_ge(n_summed, NK * (c.n + 1))
                    e.wait_ge(y2_ready, c.n + 1)
                    e.wait_ge(o_turned, c.n)
                    e.scalar_tensor_tensor(out=o[:, :], in0=ps_o[:, :], scalar=mod_col(2, c), in1=y2[:, c.q, :],
                                           op0=ALU.mult, op1=ALU.add).then_inc(o_ready, 1)

                def x1():
                    e.wait_ge(o_turned, c.n + 1)
                    if c.has(2):
                        e.wait_ge(sent[c.q], 16 * J * c.round)
                    if c.static():
                        x_c = x_in[:, c.n, :].rearrange("p (j d) -> p j d", d=D)
                    else:
                        x_c = x_in[:, bass.ds(c.n, 1), :].rearrange("p o (j d) -> p (o j) d", d=D)
                    e.tensor_tensor(row[:, c.q, :, D:2 * D], ps_x[:, :].rearrange("p (j d) -> p j d", d=D), x_c,
                                    ALU.add).then_inc(x1_ready, 1)
                    e.tensor_copy(mod_c[:, c.q, :, :], mod_r[:, bass.ds(c.round, 1), 0:2, :]
                                  .rearrange("p o s d -> p (o s) d"))

                norm2 = norm_steps(
                    c, lambda j: row[:, c.q, j, D:2 * D], stats2, mv2, ve2, nw2, v_norm2, var2_ready,
                    rstd2_ready, r02, xn2,
                    before=lambda: e.wait_ge(x1_ready, c.n + 1),
                    after=(rstd2_done, lambda: e.wait_ge(h2_ready, c.n), xn2_ready),
                    slots=(27, 28, 29, 30, 33, 34, 35, 36))

                def logit():
                    e.wait_ge(logits_ready, c.n + 1)
                    e.tensor_tensor(lg[:, :, :], ps_1[:, 0:J * E].rearrange("p (j e) -> p j e", e=E),
                                    br[:, :].unsqueeze(1).broadcast_to([P, J, E]), ALU.add).then_inc(logits_read, 1)

                def largest():
                    e.wait_ge(logits_read, c.n + 1)
                    e.tensor_reduce(mx[:, :], lg[:, :, :], AX.X, ALU.max).then_inc(v_route, 1)

                def compare():
                    top = mx[:, :].unsqueeze(2).broadcast_to([P, J, E])
                    e.wait_ge(v_route, 7 * c.n + 1)
                    e.tensor_tensor(df[:, :, :], lg[:, :, :], top, ALU.subtract).then_inc(diff_ready, 1)
                    e.tensor_tensor(eq[:, :, :], lg[:, :, :], top, ALU.is_ge).then_inc(v_route, 1)

                def score_():
                    e.wait_ge(v_route, 7 * c.n + 2)
                    e.tensor_tensor(score[:, :, :], eq[:, :, :],
                                    consts[:, C_PRI:C_PRI + J * E].rearrange("p (j e) -> p j e", e=E),
                                    ALU.mult).then_inc(v_route, 1)

                def best():
                    e.wait_ge(v_route, 7 * c.n + 3)
                    e.tensor_reduce(ms[:, :], score[:, :, :], AX.X, ALU.max).then_inc(v_route, 1)

                def choice():
                    e.wait_ge(v_route, 7 * c.n + 4)
                    top = ms[:, :].unsqueeze(2).broadcast_to([P, J, E])
                    e.tensor_tensor(oh[:, :, :], score[:, :, :], top, ALU.is_equal).then_inc(v_route, 1)
                    if c.has(1):
                        e.wait_ge(counts_ready, c.n)
                    e.tensor_tensor(ohb[:, :, :], score[:, :, :], top, ALU.is_equal).then_inc(oh_ready, 1)

                def denominator():
                    e.wait_ge(ex_ready, c.n + 1)
                    e.tensor_reduce(se[:, :], ex[:, :, :], AX.X, ALU.add).then_inc(v_route, 1)

                def gate_():
                    e.wait_ge(v_route, 7 * c.n + 6)
                    e.reciprocal(gate[:, :], se[:, :]).then_inc(v_route, 1)

                def gate_rows():
                    e.wait_ge(v_route, 7 * c.n + 7)
                    gb = mod_r[:, bass.ds(c.round, 1), 2, :].rearrange("p o d -> p (o d)")
                    for j in range(J):
                        e.tensor_scalar(row[:, c.q, j, 2 * D:3 * D], gb, gate[:, j:j + 1], None, ALU.mult)
                    e.tensor_copy(row[:, c.q, :, ROW - 1:ROW].bitcast(U32).rearrange("p j o -> p (j o)"), tok[:, :])\
                        .then_inc(v_place, 1)

                def carry():
                    e.wait_ge(v_place, 8 * c.n + 1)
                    e.tensor_scalar(tok[:, :], tok[:, :], float(CH), None, ALU.add).then_inc(tok_next, 1)
                    e.tensor_copy(base[:, 0, :], base[:, J, :]).then_inc(v_place, 1)

                def add_tile(j):
                    if j == 0:
                        e.wait_ge(counts_ready, c.n + 1)
                    e.wait_ge(v_place, 8 * c.n + 2 + j)
                    e.tensor_tensor(base[:, j + 1, :], base[:, j, :], ps_x[:, 64 + j * E:64 + (j + 1) * E], ALU.add)\
                        .then_inc(v_place, 1)

                def place_1():
                    e.wait_ge(v_place, 8 * c.n + 6)
                    e.tensor_tensor(pos[:, :, :], base[:, 0:J, :], ps_x[:, 0:J * E].rearrange("p (j e) -> p j e", e=E),
                                    ALU.add).then_inc(ranks_read, 1)

                def place_2():
                    e.wait_ge(ranks_read, c.n + 1)
                    e.tensor_tensor(picked[:, :, :], pos[:, :, :], oh[:, :, :], ALU.mult).then_inc(v_place, 1)

                def place_3():
                    e.wait_ge(v_place, 8 * c.n + 7)
                    e.tensor_reduce(slotf[:, :], picked[:, :, :], AX.X, ALU.add).then_inc(v_place, 1)

                def place_4():
                    e.wait_ge(v_place, 8 * c.n + 8)
                    e.wait_ge(tok_next, c.n + 1)
                    e.tensor_copy(slot[:, c.q, :], slotf[:, :]).then_inc(row_ready, 1)

                return ([(i + 2, lambda i=i: arg(i)) for i in range(NG)] + norm1 + norm2
                        + [(NQ * k + 8, lambda k=k: weighed(k)) for k in DVE_K]
                        + [(-20, tanh_in), (-16, lifted), (-14, relu3), (-10, softplus_in), (-7, softplus_out),
                           (-6, split_1), (-5, split_2), (-4, split_3), (-3, split_4), (-5, cb_), (-4, dx_),
                           (-1, second_term), (24, first_term), (26, x1),
                           (43, logit), (44, largest), (45, compare), (46, score_), (47, best), (48, choice),
                           (48, denominator), (49, gate_), (50, gate_rows), (51, carry), (51, lambda: add_tile(0)),
                           (52, lambda: add_tile(1)), (52, lambda: add_tile(2)), (53, lambda: add_tile(3)),
                           (53, place_1), (54, place_2), (54, place_3), (55, place_4)])

            pipeline(e, chunk_steps, **CHUNKS)
            e.wait_ge(row_ready, NCH)

            total = base[:, J, :]
            start = consts[:, C_BASE:C_BASE + E]
            then(e.tensor_scalar(pad_at[:, 0:E], total, consts[:, C_PART:C_PART + 1], None, ALU.add))
            e.tensor_scalar(pad_at[:, E:E + 1], consts[:, C_PART:C_PART + 1], float(DEAD), None, ALU.add)\
                .then_inc(pad_ready, 1)
            then(e.tensor_tensor(cnt[:, :], total, start, ALU.subtract))
            then(e.tensor_tensor(cmp[:, :, :], cnt[:, :].unsqueeze(2).broadcast_to([P, E, T // P]),
                                 consts[:, C_STEP:C_STEP + T // P].unsqueeze(1).broadcast_to([P, E, T // P]),
                                 ALU.is_gt))
            then(e.tensor_reduce(ntl[:, :], cmp[:, :, :], AX.X, ALU.add))
            then(e.tensor_copy(cum[:, 0:1], ntl[:, 0:1]))
            for x in range(1, E):
                then(e.tensor_tensor(cum[:, x:x + 1], cum[:, x - 1:x], ntl[:, x:x + 1], ALU.add))
            tiles = consts[:, C_TILE:C_TILE + NT]
            then(e.tensor_tensor(cmp2[:, :, :], tiles.unsqueeze(2).broadcast_to([P, NT, E]),
                                 cum[:, :].unsqueeze(1).broadcast_to([P, NT, E]), ALU.is_ge))
            then(e.tensor_reduce(tile_e[:, :], cmp2[:, :, :], AX.X, ALU.add))
            then(e.tensor_tensor(cmp3[:, :, :], cmp2[:, :, :], ntl[:, :].unsqueeze(1).broadcast_to([P, NT, E]),
                                 ALU.mult))
            then(e.tensor_reduce(tile_w[:, 0, :], cmp3[:, :, :], AX.X, ALU.add))
            then(e.tensor_tensor(tile_w[:, 1, :], tiles, tile_w[:, 0, :], ALU.subtract))
            then(e.tensor_scalar(tile_w[:, 2, :], tile_e[:, :], float(E), float(P), ALU.is_lt, ALU.mult))
            then(e.tensor_tensor(tile_w[:, 3, :], tile_w[:, 1, :], tile_w[:, 2, :], ALU.mult))
            then(e.scalar_tensor_tensor(out=tile_w[:, 1, :], in0=tile_e[:, :], scalar=float(REGION),
                                        in1=tile_w[:, 3, :], op0=ALU.mult, op1=ALU.add))
            then(e.tensor_copy(tile_start[:, 3:], tile_w[:, 1, :]))
            then(e.tensor_scalar(tile_expert[:, :], tile_e[:, :], float(E - 1), None, ALU.min))
            e.tensor_scalar(tile_expert_3[:, 3:], tile_e[:, :], float(E - 1), None, ALU.min).then_inc(table_ready, 1)
            e.wait_ge(table_ready, 1)
            e.wait_ge(ffn_in, 64)
            before_w, expert_w = picker(e, tile_expert, 0, 2, E - 1)
            before_b, expert_b = picker(e, tile_expert_3, 3, -1, E - 1)

            def tile_steps(t):
                def fetch():
                    x = expert_w(t)
                    if t.has(2):
                        e.wait_ge(hid_ready, t.n - 1)
                    e.tensor_copy(w1s[:, t.q % 2, :], ffn1[:, bass.ds(x, 1), :].rearrange("p o f -> p (o f)"))\
                        .then_inc(w1s_ready, 1)

                def turned():
                    e.wait_ge(xs_turned, t.n + 1)
                    if t.has(2):
                        e.wait_ge(hid_psum, t.n - 1)
                    e.tensor_copy(xst[:, t.q % 2, :], ps_d[t.q % 2][:, 0:P]).then_inc(xst_ready, 1)

                def finish_1():
                    x = expert_b(t)
                    e.wait_ge(y_psum, t.n + 1)
                    if t.has(RING):
                        e.wait_ge(stored[t.q], 16 * t.round)
                    e.tensor_tensor(ys[:, t.q, 0, :], (ps_o, ps_x)[t.q % 2][:, 0:D],
                                    ffb2[:, bass.ds(x, 1), :].rearrange("p o d -> p (o d)"), ALU.add).then_inc(v_y, 1)
                    e.tensor_copy(ids[:, t.q:t.q + 1], xs[:, t.q, ROW - 1:ROW].bitcast(U32))

                def finish_2():
                    e.wait_ge(v_y, 2 * t.n + 1)
                    e.tensor_tensor(ys[:, t.q, 1, :], ys[:, t.q, 0, :], xs[:, t.q, 2 * D:3 * D], ALU.mult)\
                        .then_inc(v_y, 1)

                def finish_3():
                    e.wait_ge(v_y, 2 * t.n + 2)
                    e.tensor_tensor(ys[:, t.q, 0, :], ys[:, t.q, 1, :], xs[:, t.q, D:2 * D], ALU.add)\
                        .then_inc(y_ready, 1)
                return [(-6, fetch), (-3, turned), (7, finish_1), (8, finish_2), (9, finish_3)]

            def before(i):
                before_w(i)
                before_b(i)
            pipeline(e, tile_steps, before=before, **TILES)

        @block.gpsimd
        def _(e):
            e.wait_ge(setup_v, 3)
            naught = e.alloc_register("naught")
            last_row = e.alloc_register("last_row")
            e.reg_mov(naught, 0)

            def chunk_steps(c):
                def weighed(k):
                    e.wait_ge(g_ready, NK * c.n + k + 1)
                    e.tensor_tensor(u[:, k, :, :], u[:, k, :, :],
                                    crep[:, c.q, :].unsqueeze(1).broadcast_to([P, NQ, CH]), ALU.mult)\
                        .then_inc(w_pool, 1)

                def h2():
                    e.wait_ge(xn2_ready, c.n + 1)
                    e.tensor_tensor(hm[:, :, :], xn2[:, :, :],
                                    mod_c[:, c.q, 1, :].unsqueeze(1).broadcast_to([P, J, D]), ALU.mult)\
                        .then_inc(pool_own, 1)
                    e.wait_ge(pool_own, c.n + 1)
                    e.tensor_tensor(row[:, c.q, :, 0:D], hm[:, :, :],
                                    mod_c[:, c.q, 0, :].unsqueeze(1).broadcast_to([P, J, D]), ALU.add)\
                        .then_inc(h2_ready, 1)

                def send():
                    e.wait_ge(row_ready, c.n + 1)
                    e.wait_ge(h2_ready, c.n + 1)
                    e.reg_add(last_row, naught, E * REGION + P - 1)
                    for j in range(J):
                        e.indirect_dma_start(rows, bass.IndirectOffsetOnAxis(ap=slot[:, c.q, j:j + 1], axis=0),
                                             row[:, c.q, j, :], None, bounds_check=last_row,
                                             oob_is_err=True).then_inc(sent[c.q], 16)
                return [(NQ * k + 8, lambda k=k: weighed(k)) for k in POOL_K] + [(37, h2), (56, send)]
            pipeline(e, chunk_steps, **CHUNKS)

            e.wait_ge(pad_ready, 1)
            e.reg_add(last_row, naught, E * REGION + P - 1)
            for x in range(E + 1):
                e.indirect_dma_start(rows, bass.IndirectOffsetOnAxis(ap=pad_at[:, x:x + 1], axis=0), pad[:, :],
                                     None, bounds_check=last_row, oob_is_err=True).then_inc(pad_sent, 16)

            def store(t):
                e.wait_ge(y_ready, t.n + 1)
                e.reg_add(last_row, naught, T - 1)
                e.indirect_dma_start(out, bass.IndirectOffsetOnAxis(ap=ids[:, t.q:t.q + 1], axis=0),
                                     ys[:, t.q, 0, :], None, bounds_check=last_row, oob_is_err=False)\
                    .then_inc(stored[t.q], 16)
            pipeline(e, lambda t: [(10, lambda: store(t))], **TILES)
            for q in range(RING):
                e.wait_ge(stored[q], 16 * NT // RING)


def shape_constants(np):
    k = np.zeros((P, C_ALL), np.float32)
    p = np.arange(P)
    k[:, C_ID:C_ID + P] = np.eye(P)
    k[:, C_TRI:C_TRI + P] = p[:, None] < p[None, :]
    n, d8 = p // DG, p % DG
    for b in range(NK):
        k[0:96, C_SEL + b * P:C_SEL + (b + 1) * P] = (np.arange(96)[:, None] % 32) == (DG * b + d8)[None, :]
        for q in range(NQ):
            at = C_MASK + (NK * q + b) * 32
            k[:, at:at + 32] = np.arange(32)[None, :] == (DG * b + d8)[:, None]
    k[:, C_PRI:C_PRI + J * E] = np.tile(E - np.arange(E), J)
    k[:, C_BASE:C_BASE + E] = np.arange(E) * REGION
    k[:, C_TILE:C_TILE + NT] = np.arange(NT)
    k[:, C_STEP:C_STEP + T // P] = np.arange(T // P) * P
    k[:, C_PART] = p
    k[:, C_TOK:C_TOK + J] = p[:, None] * J + np.arange(J)
    return k


def kernel(**inputs):
    import numpy as np
    import concourse.bacc as bacc
    from concourse.bass_utils import run_bass_kernel_spmd

    v = {n: np.asarray(x) for n, x in inputs.items()}

    def by_group(m):
        return m.reshape(D // DG, DG, N).transpose(2, 1, 0).reshape(P, D // DG)

    def col(x):
        return x.reshape(-1, 1)

    smalls = np.concatenate(
        [by_group(v["L0_attn_A"]), by_group(v["L0_attn_state_init"][0]),
         col(np.repeat(v["L0_attn_b2"], DG)), col(np.repeat(v["L0_attn_b3"], DG)), col(v["L0_attn_b1"]),
         col(v["L0_attn_bl1"]), col(v["L0_attn_bl2"]), col(v["L0_attn_bf1"]), col(v["L0_attn_bf2"])], axis=1)
    arrays = {
        "x": v["L0_attn_x"].reshape(NCH, P, J * D),
        "consts": shape_constants(np),
        "smalls": smalls,
        "W1": v["L0_attn_W1"], "W2": v["L0_attn_W2"], "W3": v["L0_attn_W3"],
        "Wl1": v["L0_attn_Wl1"], "Wl2": v["L0_attn_Wl2"], "Wf1": v["L0_attn_Wf1"], "Wf2": v["L0_attn_Wf2"],
        "Wr": v["L0_ffn_Wr"], "br": v["L0_ffn_br"],
        "cT": v["L0_c"].T, "wmod": v["L0_wmod"],
        "ffn_W1": v["L0_ffn_W1"].transpose(1, 0, 2),
        "ffn_b1": v["L0_ffn_b1"].reshape(E, FC, P).transpose(2, 0, 1),
        "ffn_W2": v["L0_ffn_W2"].reshape(E, FC, P, D).transpose(2, 0, 1, 3),
        "ffn_b2": v["L0_ffn_b2"],
    }
    nc = bacc.Bacc("TRN2", target_bir_lowering=False, num_devices=1)
    arrays = {n + "_dram": np.ascontiguousarray(x) for n, x in arrays.items()}
    args = {n[:-5]: nc.dram_tensor(n, x.shape, F32, kind="ExternalInput").ap() for n, x in arrays.items()}
    out = nc.dram_tensor("out_dram", [T, D], F32, kind="ExternalOutput").ap()
    build(nc, args, out)
    r = run_bass_kernel_spmd(nc, [arrays], core_ids=[0])
    return r.results[0]["out_dram"].reshape(B, L, D)
```

```python
from contextlib import ExitStack

import concourse.bass as bass
from concourse import mybir

ALU = mybir.AluOpType
ACT = mybir.ActivationFunctionType
AX = mybir.AxisListType
F32 = mybir.dt.float32
BF16 = mybir.dt.bfloat16
U32 = mybir.dt.uint32
I32 = mybir.dt.int32

P = 128
B, L, D = 8, 1024, 128
N = 16
E = 8
F = 512
FC = F // P
T = B * L
CH = 512
J = CH // P
NCH = T // CH
CPB = L // CH
assert CPB == 2
DG = P // N
NQ = 4
NK = D // DG // NQ
REGION = P + T
NT = T // P + E
ROUND = float(1 << 23)
NO_TOKEN = 1 << 20
ROW = 3 * D + 1
EPS = 1e-5
TANH_CLAMP = 20.0
SOFTPLUS_CLAMP = 30.0
W1C = F + FC + D

C_ID = 0
C_TRI = C_ID + P
C_SEL = C_TRI + P
C_MASK = C_SEL + NK * P
C_PRI = C_MASK + NK * NQ * 32
C_BASE = C_PRI + J * E
C_TILE = C_BASE + E
C_LOW = C_TILE + NT
C_PART = C_LOW + E * E
C_TOK = C_PART + 1
C_ALL = C_TOK + J

MASKED = NK * NQ * 32

SLOTS = 16
TILE_SLOTS = 4
RING = 8


class Item:

    def __init__(self, n, q, ring, round):
        self.n, self.q, self.ring, self.round = n, q, ring, round

    def static(self):
        return isinstance(self.n, int)

    def has(self, k):
        return not self.static() or self.n >= k

    def at(self, k):
        q = self.q + k
        return Item(self.n + k, q % self.ring, self.ring, self.round + q // self.ring)


def pipeline(engine, steps_of, total, slots, ring, loop_from, rounds, turns, before=None, once=()):
    def turn(item):
        found = [(slot - item.n * slots, -1, step) for slot, step in once
                 if item.static() and item.n * slots <= slot < (item.n + 1) * slots]
        for k in range(-4, 5):
            other = item.at(-k)
            if item.static() and not 0 <= other.n < total:
                continue
            found += [(slot - k * slots, order, step) for order, (slot, step) in enumerate(steps_of(other))
                      if k * slots <= slot < (k + 1) * slots]
        for _, _, step in sorted(found, key=lambda x: x[0]):
            step()

    def peeled(ns):
        for n in ns:
            turn(Item(n, n % ring, ring, n // ring))

    peeled(range(turns[0], loop_from))
    with engine.Fori(0, rounds) as i:
        if before:
            before(i)
        for k in range(ring):
            turn(Item(i * ring + (loop_from + k), (loop_from + k) % ring, ring, i + (loop_from + k) // ring))
    peeled(range(loop_from + rounds * ring, turns[1]))


def build(nc, a, out):
    with ExitStack() as ctx:
        def sb(name, shape, dt=F32):
            return ctx.enter_context(nc.sbuf_tensor(name, shape, dt))

        def ps(name):
            return ctx.enter_context(nc.psum_tensor(name, [P, CH], F32))

        def sem(name):
            return ctx.enter_context(nc.semaphore(name))

        rows = nc.dram_tensor("rows", [E * REGION, ROW], F32, kind="Internal").ap()

        consts = sb("consts", [P, C_ALL])
        ident = consts[:, C_ID:C_ID + P]
        tri = sb("tri", [P, P], BF16)
        ones_bf = sb("ones_bf", [P, P], BF16)
        eighth = sb("eighth", [P, P])
        sel = sb("sel", [96, NK, P], BF16)
        hsel = sb("hsel", [P, NQ * NK, 32])
        smalls = sb("smalls", [P, 2 * N + 7])
        a_r = smalls[:, 0:N]
        h0_r = smalls[:, N:2 * N]
        a_neg = sb("a_neg", [P, N])
        a_pos = sb("a_pos", [P, N])
        b2r = smalls[:, 2 * N:2 * N + 1]
        b3r = smalls[:, 2 * N + 1:2 * N + 2]
        b1 = smalls[:, 2 * N + 2:2 * N + 3]
        bl1 = smalls[:, 2 * N + 3:2 * N + 4]
        bl2 = smalls[:, 2 * N + 4:2 * N + 5]
        bf1 = smalls[:, 2 * N + 5:2 * N + 6]
        bf2 = smalls[:, 2 * N + 6:2 * N + 7]
        w1 = sb("w1", [P, D])
        wl1 = sb("wl1", [P, D])
        wl2 = sb("wl2", [P, D])
        wf1 = sb("wf1", [P, 2, D])
        wf1_neg2 = sb("wf1_neg2", [P, D])
        bf1_all = sb("bf1_all", [P, 1])
        ones = sb("ones", [P, 1])
        wf2 = sb("wf2", [P, D])
        w23 = sb("w23", [P, 2, N])
        w2r = sb("w2r", [P, N, DG])
        w3r = sb("w3r", [P, N, DG])
        wr = sb("wr", [P, E])
        br = sb("br", [P, E])
        ffn1 = sb("ffn1", [P, E, W1C])
        ffn2 = sb("ffn2", [P, E, FC, D])
        ct = sb("ct", [P, B])
        c_work = sb("c_work", [P, 3, B])
        sc = sb("sc", [P, B])
        wmod = sb("wmod", [P, 6, D])
        mod_t = sb("mod_t", [P, 3, B])
        mod_g = sb("mod_g", [P, 2, B])
        mod_r = sb("mod_r", [P, B, 3, D])

        x_in = sb("x_in", [P, NCH, J * D])
        stats = sb("stats", [P, J, 6])
        mv = sb("mv", [P, 6, J])
        ve = sb("ve", [P, J])
        lnv = sb("lnv", [P, J])
        r0 = sb("r0", [P, J])
        nw = sb("nw", [P, 3, J])
        xn = sb("xn", [P, J, D])
        h1t = sb("h1t", [P, CH])
        a1 = sb("a1", [P, CH])
        th = sb("th", [P, 2, CH])
        a3 = sb("a3", [P, CH])
        xt = sb("xt", [P, CH])
        sp = sb("sp", [P, 2, CH])
        delta = sb("delta", [P, CH])
        crep = sb("crep", [P, 2, CH])
        cb = sb("cb", [P, CH])
        dx = sb("dx", [P, CH])
        y2 = sb("y2", [P, 2, CH])
        part = sb("part", [P, 3, CH], BF16)
        rest = sb("rest", [P, CH])
        stk = sb("stk", [96, 2, NQ, CH], BF16)
        u = sb("u", [P, NK, NQ, CH])
        o = sb("o", [P, CH])
        stats2 = sb("stats2", [P, J, 6])
        mv2 = sb("mv2", [P, 6, J])
        ve2 = sb("ve2", [P, J])
        lnv2 = sb("lnv2", [P, J])
        r02 = sb("r02", [P, J])
        nw2 = sb("nw2", [P, 4, J])
        xn2 = sb("xn2", [P, J, D])
        mod_c = sb("mod_c", [P, 2, D])
        hm = sb("hm", [P, J, D])
        h2t = sb("h2t", [P, CH])
        row = sb("row", [P, 2, J, ROW])
        lg = sb("lg", [P, J, E])
        mx = sb("mx", [P, J])
        df = sb("df", [P, J, E])
        ex = sb("ex", [P, J, E])
        se = sb("se", [P, J])
        gate = sb("gate", [P, J])
        score = sb("score", [P, J, E])
        picked = sb("picked", [P, J, E])
        ms = sb("ms", [P, J])
        oh = sb("oh", [P, J, E], BF16)
        base = sb("base", [P, 2, E])
        pos = sb("pos", [P, J, E])
        slotf = sb("slotf", [P, J])
        slot = sb("slot", [P, 2, J], U32)
        tok = sb("tok", [P, J])
        pad = sb("pad", [P, ROW])
        cnt = sb("cnt", [P, 3, E])
        step = sb("step", [P, 2, E - 1])
        below = sb("below", [P, E, E])
        ntl = sb("ntl", [P, E])
        cum = sb("cum", [P, E])
        tile_w = sb("tile_w", [P, 5, NT])
        tile_expert = sb("tile_expert", [P, NT], I32)
        tile_start = sb("tile_start", [P, NT + 3], I32)
        room = u[:, :, :, :].rearrange("p k q c -> p (k q c)")
        taken = [0]

        def in_u(*shape):
            n = 1
            for x in shape:
                n *= x
            v = room[:, taken[0]:taken[0] + n]
            taken[0] += n
            names = "abc"[:len(shape)]
            return v.rearrange(f"p ({' '.join(names)}) -> p {' '.join(names)}", **dict(zip(names, shape)))
        past = in_u(2, NT, E - 1)
        taken[0] = 0
        xs = in_u(RING, ROW)
        xst = in_u(2, P)
        hid = in_u(2, FC, P)
        ys = in_u(RING, 2, D)
        assert taken[0] <= NK * NQ * CH
        w1s = x_in[:, :, :].rearrange("p c t -> p (c t)")[:, 0:4 * W1C].rearrange("p (q f) -> p q f", q=4)
        w2s = x_in[:, :, :].rearrange("p c t -> p (c t)")[:, 4 * W1C:4 * (W1C + F)]\
            .rearrange("p (q f d) -> p q f d", q=4, f=FC)
        setup_room = row[:, :, :, :].rearrange("p q j r -> p (q j r)")
        sc_rep = setup_room[:, 0:B * P].rearrange("p (b m) -> p b m", b=B)
        g_work = setup_room[:, B * P:B * P + 2 * B * D].rearrange("p (i m) -> p i m", i=2)

        ps_0 = ps("ps_0")
        ps_1 = ps("ps_1")
        ps_2 = ps("ps_2")
        ps_d = [ps("ps_d0"), ps("ps_d1"), ps("ps_d2")]
        ps_o = ps("ps_o")
        ps_x = ps("ps_x")

        w_in = sem("w_in")
        ffn_in = sem("ffn_in")
        setup_v = sem("setup_v")
        setup_a = sem("setup_a")
        setup_p = sem("setup_p")
        setup_g = sem("setup_g")
        setup_chain = sem("setup_chain")
        x_here = [sem("x_here0"), sem("x_here1"), sem("x_here2")]
        v_norm = sem("v_norm")
        var_ready = sem("var_ready")
        var_log = sem("var_log")
        tanh_exp = sem("tanh_exp")
        tanh_log = sem("tanh_log")
        sp_exp = sem("sp_exp")
        rstd_ready = sem("rstd_ready")
        rstd_done = sem("rstd_done")
        xn_ready = sem("xn_ready")
        xn_turned = sem("xn_turned")
        h1_ready = sem("h1_ready")
        z1_ready = sem("z1_ready")
        a1_ready = sem("a1_ready")
        z2_ready = sem("z2_ready")
        tanh_arg = sem("tanh_arg")
        tanh_ready = sem("tanh_ready")
        z3_ready = sem("z3_ready")
        a3_ready = sem("a3_ready")
        z4_ready = sem("z4_ready")
        xt_ready = sem("xt_ready")
        z5_ready = sem("z5_ready")
        zc_ready = sem("zc_ready")
        zb_ready = sem("zb_ready")
        sp_arg = sem("sp_arg")
        sp_log = sem("sp_log")
        delta_ready = sem("delta_ready")
        v_split = sem("v_split")
        c_ready = sem("c_ready")
        cb_ready = sem("cb_ready")
        s_ready = sem("s_ready")
        y2_ready = sem("y2_ready")
        parts_ready = sem("parts_ready")
        stk_here = [sem("stk_here0"), sem("stk_here1")]
        rep_ready = sem("rep_ready")
        e_ready = sem("e_ready")
        arg_ready = sem("arg_ready")
        g_ready = sem("g_ready")
        w_pool = sem("w_pool")
        w_dve = sem("w_dve")
        n_summed = sem("n_summed")
        o_ready = sem("o_ready")
        o_turned = sem("o_turned")
        x1_ready = sem("x1_ready")
        v_norm2 = sem("v_norm2")
        var2_ready = sem("var2_ready")
        var2_log = sem("var2_log")
        rstd2_ready = sem("rstd2_ready")
        rstd2_done = sem("rstd2_done")
        xn2_ready = sem("xn2_ready")
        shift_ready = sem("shift_ready")
        part0_ready = sem("part0_ready")
        dx_ready = sem("dx_ready")
        base_ready = sem("base_ready")
        pool_own = sem("pool_own")
        h2_ready = sem("h2_ready")
        h2_turned = sem("h2_turned")
        h2t_ready = sem("h2t_ready")
        logits_ready = sem("logits_ready")
        v_route = sem("v_route")
        logits_read = sem("logits_read")
        diff_ready = sem("diff_ready")
        ex_ready = sem("ex_ready")
        oh_ready = sem("oh_ready")
        counts_ready = sem("counts_ready")
        v_place = sem("v_place")
        ranks_read = sem("ranks_read")
        tok_next = sem("tok_next")
        row_ready = sem("row_ready")
        sent = [sem("sent0"), sem("sent1")]
        pad_ready = sem("pad_ready")
        pad_sent = sem("pad_sent")
        table_ready = sem("table_ready")
        xs_here = [sem(f"xs_here{i}") for i in range(RING)]
        xs_turned = sem("xs_turned")
        xst_ready = sem("xst_ready")
        w1s_ready = sem("w1s_ready")
        w2s_ready = sem("w2s_ready")
        hid_psum = sem("hid_psum")
        hid_ready = sem("hid_ready")
        y_psum = sem("y_psum")
        v_y = sem("v_y")
        y_ready = sem("y_ready")
        stored = [sem(f"stored{i}") for i in range(RING)]

        NG = NK * NQ
        POOL_K = (0, 1, 2)
        DVE_K = (3,)
        CHUNKS = dict(total=NCH, slots=SLOTS, ring=2, loop_from=3, rounds=5, turns=(-3, NCH + 4))
        TILES = dict(total=NT, slots=TILE_SLOTS, ring=RING, loop_from=6, rounds=(NT - 9) // RING,
                     turns=(-4, NT + 4))
        assert 3 + 5 * 2 <= NCH - 3

        block = ctx.enter_context(nc.Block())

        N_W = 13
        y_banks = (ps_o, ps_x, ps_2, ps_d[2])

        def load_eight(e, table, at, limit):
            _, values = nc.values_load_multi_w_load_instructions(
                table[0:1, bass.ds(at, RING)], engines=[e.engine], min_val=0, max_val=limit)
            return values

        def picker(e, table, shift, ahead, limit):
            now = []

            def before(i):
                now[:] = load_eight(e, table, i * RING + (TILES["loop_from"] + ahead + shift), limit)

            def pick(t):
                if t.static():
                    return e.value_load(table[0:1, t.n + shift:t.n + shift + 1], min_val=0, max_val=limit)
                return now[(t.q - TILES["loop_from"] - ahead) % RING]
            return before, pick

        def mod_col(s, c):
            return mod_t[:, s, bass.ds(c.round, 1)]

        def x_of(c, j):
            if c.static():
                return x_in[:, c.n, j * D:(j + 1) * D]
            return x_in[:, bass.ds(c.n, 1), j * D:(j + 1) * D].rearrange("p o d -> p (o d)")

        def bank(i):
            return i % 3 if i < NG - 1 else 1

        @block.sync
        def _(e):
            def load(dst, src):
                e.dma_start(dst, src).then_inc(w_in, 16)
            e.dma_start(x_in[:, 0, :], a["x"][0]).then_inc(x_here[0], 16)
            load(smalls[:, :], a["smalls"])
            load(ct[:, :], a["cT"])
            load(wmod[:, :, :], a["wmod"].rearrange("p (s d) -> p s d", s=6))
            load(consts[:, :], a["consts"])
            load(wl1[:, :], a["Wl1"])
            load(wl2[:, :], a["Wl2"])
            load(wf1[:, :, :], a["Wf1"].rearrange("(c p) h -> p c h", p=P))
            load(wf2[:, :], a["Wf2"])
            load(w1[:, :], a["W1"])
            load(w23[:, 0, :], a["W2"])
            load(w23[:, 1, :], a["W3"])
            load(wr[:, :], a["Wr"])
            load(br[:, :], a["br"].rearrange("(o e) -> o e", o=1).to_broadcast([P, E]))
            e.dma_start(x_in[:, 1, :], a["x"][1]).then_inc(x_here[1], 16)
            e.dma_start(x_in[:, 2:NCH, :], a["x"][2:NCH].rearrange("c p t -> p c t")).then_inc(x_here[2], 16)
            e.dma_start(ffn2[:, :, :, :], a["ffn_W2"]).then_inc(ffn_in, 16)
            e.dma_start(ffn1[:, :, 0:F], a["ffn_W1"]).then_inc(ffn_in, 16)
            e.dma_start(ffn1[:, :, F:F + FC], a["ffn_b1"]).then_inc(ffn_in, 16)
            e.dma_start(ffn1[:, :, F + FC:W1C], a["ffn_b2"].rearrange("(o e) d -> o e d", o=1)
                        .to_broadcast([P, E, D])).then_inc(ffn_in, 16)
            e.wait_ge(pad_ready, 1)
            for x in range(E):
                e.dma_start(rows[x * REGION:x * REGION + P, :], pad[:, :]).then_inc(pad_sent, 16)

            def stack(c):
                e.wait_ge(parts_ready, c.n + 1)
                if c.has(2):
                    e.wait_ge(rep_ready, (c.n - 1) * NG)
                for k in range(3):
                    for qd in range(NQ):
                        e.dma_start(stk[32 * k:32 * k + 32, c.q, qd, :], part[32 * qd:32 * qd + 32, k, :])\
                            .then_inc(stk_here[c.q], 16)
            pipeline(e, lambda c: [(-8, lambda: stack(c))], **CHUNKS)

            e.wait_ge(table_ready, 1)
            e.wait_ge(sent[0], 16 * J * NCH // 2)
            e.wait_ge(sent[1], 16 * J * NCH // 2)
            e.wait_ge(pad_sent, 16 * E)
            before, start_of = picker(e, tile_start, 3, 3, E * REGION - P)

            def tile_load(t):
                start = start_of(t)
                if t.has(RING):
                    e.wait_ge(stored[t.q], 16 * t.round)
                e.dma_start(xs[:, t.q, :], rows[bass.ds(start, P), :]).then_inc(xs_here[t.q], 16)
            pipeline(e, lambda t: [(-12, lambda: tile_load(t))], before=before, **TILES)

        @block.scalar
        def _(e):
            e.preload_act_table_set("natural_log_exp_and_others")

            def silu_exp():
                e.wait_ge(w_in, 16 * N_W)
                e.activation(c_work[:, 0, :], ct[:, :], ACT.Exp, scale=-1.0).then_inc(setup_a, 1)

            def chunk_steps(c):
                def ln_var():
                    e.wait_ge(var_ready, c.n + 1)
                    e.activation(lnv[:, :], ve[:, :], ACT.Ln).then_inc(var_log, 1)

                def rstd():
                    e.wait_ge(var_log, c.n + 1)
                    e.activation(r0[:, :], lnv[:, :], ACT.Exp, scale=-0.5).then_inc(rstd_ready, 1)

                def h1():
                    e.wait_ge(xn_turned, c.n + 1)
                    e.wait_ge(z3_ready, c.n)
                    e.activation(h1t[:, :], ps_2[:, :], ACT.Identity, bias=mod_col(0, c), scale=mod_col(1, c))\
                        .then_inc(h1_ready, 1)

                def a1_():
                    e.wait_ge(z1_ready, c.n + 1)
                    e.activation(a1[:, :], ps_0[:, :], ACT.Relu, bias=bl1).then_inc(a1_ready, 1)

                def tanh_1():
                    e.wait_ge(tanh_arg, c.n + 1)
                    e.wait_ge(z3_ready, c.n)
                    e.activation(th[:, 1, :], th[:, 0, :], ACT.Exp, scale=2.0).then_inc(tanh_exp, 1)

                def tanh_2():
                    e.wait_ge(tanh_exp, c.n + 1)
                    e.activation(th[:, 0, :], th[:, 1, :], ACT.Ln, bias=1.0).then_inc(tanh_log, 1)

                def tanh_3():
                    e.wait_ge(tanh_log, c.n + 1)
                    e.activation(th[:, 1, :], th[:, 0, :], ACT.Exp, scale=-1.0).then_inc(tanh_ready, 1)

                def a3_():
                    e.wait_ge(z3_ready, c.n + 1)
                    e.wait_ge(z4_ready, c.n)
                    e.activation(a3[:, :], ps_1[:, :], ACT.Relu, bias=bf1_all[:, :]).then_inc(a3_ready, 1)

                def x_trans():
                    e.wait_ge(z4_ready, c.n + 1)
                    e.wait_ge(zb_ready, c.n)
                    e.wait_ge(y2_ready, c.n)
                    e.activation(xt[:, :], ps_0[:, :], ACT.Identity, bias=bf2).then_inc(xt_ready, 1)

                def c_rep():
                    e.wait_ge(zc_ready, c.n + 1)
                    if c.has(2):
                        e.wait_ge(w_pool, len(POOL_K) * (c.n - 1))
                        e.wait_ge(w_dve, len(DVE_K) * (c.n - 1))
                    e.activation(crep[:, c.q, :], ps_1[:, :], ACT.Identity, bias=b3r).then_inc(c_ready, 1)

                def softplus_1():
                    e.wait_ge(sp_arg, c.n + 1)
                    e.activation(sp[:, 1, :], sp[:, 0, :], ACT.Exp).then_inc(sp_exp, 1)

                def softplus_2():
                    e.wait_ge(sp_exp, c.n + 1)
                    e.activation(sp[:, 0, :], sp[:, 1, :], ACT.Ln, bias=1.0).then_inc(sp_log, 1)

                def part_0():
                    e.wait_ge(delta_ready, c.n + 1)
                    if c.q == 1:
                        e.wait_ge(stk_here[0], 16 * 3 * NQ * (c.round + 1))
                    elif c.has(1):
                        e.wait_ge(stk_here[1], 16 * 3 * NQ * c.round)
                    e.activation(part[:, 0, :], delta[:, :], ACT.Copy).then_inc(part0_ready, 1)

                def exp_1(i):
                    k, qd = i // NQ, i % NQ
                    e.wait_ge(rep_ready, NG * c.n + i + 1)
                    if qd == 0 and c.has(1):
                        e.wait_ge(n_summed, NK * (c.n - 1) + k + 1)
                    e.activation(u[:, k, qd, :], ps_d[bank(i)][:, :], ACT.Exp,
                                 scale=a_neg[:, NK * qd + k:NK * qd + k + 1]).then_inc(e_ready, 1)

                def exp_2(k):
                    e.wait_ge(arg_ready, NG * c.n + NQ * (k + 1))
                    e.activation(u[:, k, :, :], u[:, k, :, :], ACT.Exp, scale=-1.0, bias=1.0).then_inc(g_ready, 1)

                def x1():
                    e.wait_ge(o_turned, c.n + 1)
                    if c.has(2):
                        e.wait_ge(sent[c.q], 16 * J * c.round)
                    e.activation(row[:, c.q, :, D:2 * D], ps_x[:, :].rearrange("p (j d) -> p j d", d=D), ACT.Copy)\
                        .then_inc(x1_ready, 1)

                def normed2():
                    e.wait_ge(shift_ready, c.n + 1)
                    e.wait_ge(h2_ready, c.n)
                    for j in range(J):
                        ins = e.activation(xn2[:, j, :], row[:, c.q, j, D:2 * D], ACT.Identity,
                                           bias=nw2[:, 3, j:j + 1], scale=nw2[:, 2, j:j + 1])
                    ins.then_inc(xn2_ready, 1)

                def ln_var2():
                    e.wait_ge(var2_ready, c.n + 1)
                    e.activation(lnv2[:, :], ve2[:, :], ACT.Ln).then_inc(var2_log, 1)

                def rstd2():
                    e.wait_ge(var2_log, c.n + 1)
                    e.activation(r02[:, :], lnv2[:, :], ACT.Exp, scale=-0.5).then_inc(rstd2_ready, 1)

                def h2():
                    e.wait_ge(h2_turned, c.n + 1)
                    e.wait_ge(logits_ready, c.n)
                    e.activation(h2t[:, :], ps_x[:, :], ACT.Copy).then_inc(h2t_ready, 1)

                def probs():
                    e.wait_ge(diff_ready, c.n + 1)
                    e.activation(ex[:, :, :], df[:, :, :], ACT.Exp).then_inc(ex_ready, 1)
                return ([(i + 1, lambda i=i: exp_1(i)) for i in range(NG)]
                        + [(NQ * k + 6, lambda k=k: exp_2(k)) for k in range(NK)]
                        + [(-38, ln_var), (-37, rstd), (-30, h1), (-28, a1_), (-25, tanh_1), (-24, tanh_2),
                           (-23, tanh_3), (-20, a3_), (-18, x_trans), (-15, softplus_1), (-14, softplus_2), (-12, part_0), (-11, c_rep),
                           (26, x1), (31, ln_var2), (32, rstd2), (36.5, normed2), (40, h2), (44.5, probs)])
            pipeline(e, chunk_steps, once=[(-32.5, silu_exp),
                                           (-30.5, lambda: e.wait_ge(setup_v, 2)),
                                           (-20.5, lambda: e.wait_ge(setup_v, 3))],
                     **CHUNKS)

            def turned(t):
                e.wait_ge(xs_turned, t.n + 1)
                if t.has(2):
                    e.wait_ge(hid_psum, t.n - 1)
                e.activation(xst[:, t.q % 2, :], ps_d[t.q % 2][:, 0:P], ACT.Copy).then_inc(xst_ready, 1)

            def gelu(t):
                e.wait_ge(hid_psum, t.n + 1)
                if t.has(2):
                    e.wait_ge(y_psum, t.n - 1)
                for f in range(FC):
                    ins = e.activation(hid[:, t.q % 2, f, :], (ps_0, ps_1)[t.q % 2][:, f * P:(f + 1) * P], ACT.Gelu,
                                       bias=w1s[:, t.q % 4, F + f:F + f + 1])
                ins.then_inc(hid_ready, 1)
            pipeline(e, lambda t: [(-3, lambda: turned(t)), (2, lambda: gelu(t))], **TILES)

        @block.tensor
        def _(e):
            def columns():
                e.wait_ge(setup_v, 1)
                for s in range(3):
                    e.matmul(ps_x[:, s * B:(s + 1) * B], wmod[:, s, :], sc[:, :], start=True, stop=True)
                e.matmul(ps_x[:, 3 * B:3 * B + 1], wf1[:, 1, :], ones[:, :], start=True, stop=True)\
                    .then_inc(setup_p, 1)

            def rows_of(b):
                if b < 2:
                    e.wait_ge(setup_v, 2)
                else:
                    e.wait_ge(setup_g, b - 1)
                e.matmul((ps_o, ps_x)[b % 2][:, 0:3 * D], sc_rep[:, b, :], wmod[:, 3:6, :], start=True, stop=True)\
                    .then_inc(setup_p, 1)

            def chunk_steps(c):
                def turn():
                    e.wait_ge(xn_ready, c.n + 1)
                    if c.has(2):
                        e.wait_ge(y2_ready, c.n - 1)
                    for j in range(J):
                        ins = e.transpose(ps_2[:, j * P:(j + 1) * P], xn[:, j, :], ident)
                    ins.then_inc(xn_turned, 1)

                def z1():
                    e.wait_ge(h1_ready, c.n + 1)
                    e.wait_ge(xt_ready, c.n)
                    e.matmul(ps_0[:, :], wl1[:, :], h1t[:, :], start=True, stop=True).then_inc(z1_ready, 1)

                def z2():
                    e.wait_ge(a1_ready, c.n + 1)
                    e.matmul(ps_0[:, :], wl2[:, :], a1[:, :], start=True, stop=True).then_inc(z2_ready, 1)

                def z3():
                    e.wait_ge(tanh_ready, c.n + 1)
                    e.wait_ge(c_ready, c.n)
                    if c.has(4):
                        e.wait_ge(logits_read, c.n - 3)
                    e.matmul(ps_1[:, :], wf1[:, 0, :], h1t[:, :], start=True, stop=False)
                    e.matmul(ps_1[:, :], wf1_neg2[:, :], th[:, 1, :], start=False, stop=True).then_inc(z3_ready, 1)

                def z4():
                    e.wait_ge(a3_ready, c.n + 1)
                    e.matmul(ps_0[:, :], wf2[:, :], a3[:, :], start=True, stop=True).then_inc(z4_ready, 1)

                def z5():
                    e.wait_ge(xt_ready, c.n + 1)
                    e.matmul(ps_1[:, :], w1[:, :], xt[:, :], start=True, stop=True).then_inc(z5_ready, 1)

                def zc():
                    e.wait_ge(delta_ready, c.n + 1)
                    e.matmul(ps_1[:, :], w3r[:, :, :].rearrange("p n d -> p (n d)"), xt[:, :],
                             start=True, stop=True).then_inc(zc_ready, 1)

                def zb():
                    if not c.static() or c.n + 1 < NCH:
                        e.wait_ge(h1_ready, c.n + 2)
                    e.matmul(ps_2[:, :], w2r[:, :, :].rearrange("p n d -> p (n d)"), xt[:, :],
                             start=True, stop=True).then_inc(zb_ready, 1)

                def s():
                    e.wait_ge(cb_ready, c.n + 1)
                    e.matmul(ps_2[:, :], eighth[:, :], cb[:, :], start=True, stop=True).then_inc(s_ready, 1)

                def rep(i):
                    if i == 0:
                        e.wait_ge(stk_here[c.q], (c.round + 1) * 16 * 3 * NQ)
                    last = max(g for g in range(-NG, i) if bank(g % NG) == bank(i))
                    if last >= 0 or c.has(1):
                        e.wait_ge(arg_ready, NG * c.n + last + 1)
                    e.matmul(ps_d[bank(i)][:, :], sel[:, i // NQ, :], stk[:, c.q, i % NQ, :], start=True, stop=True)\
                        .then_inc(rep_ready, 1)

                def summed(k):
                    if k in POOL_K:
                        e.wait_ge(w_pool, len(POOL_K) * c.n + POOL_K.index(k) + 1)
                    else:
                        e.wait_ge(w_dve, len(DVE_K) * c.n + DVE_K.index(k) + 1)
                    if k == 0:
                        e.wait_ge(o_ready, c.n)
                    for qd in range(NQ):
                        ins = e.matmul(ps_o[32 * qd:32 * qd + 32, :], hsel[:, NK * qd + k, :], u[:, k, qd, :],
                                       start=(k == 0), stop=(k == NK - 1))
                    ins.then_inc(n_summed, 1)

                def turn_o():
                    e.wait_ge(o_ready, c.n + 1)
                    if c.has(1):
                        e.wait_ge(h2t_ready, c.n)
                    for j in range(J):
                        e.matmul(ps_x[:, j * P:(j + 1) * P], ident, x_of(c, j), start=True, stop=False)
                        ins = e.matmul(ps_x[:, j * P:(j + 1) * P], o[:, j * P:(j + 1) * P], ident,
                                       start=False, stop=True)
                    ins.then_inc(o_turned, 1)

                def turn_h2():
                    e.wait_ge(h2_ready, c.n + 1)
                    e.wait_ge(x1_ready, c.n + 1)
                    if c.has(1):
                        e.wait_ge(ranks_read, c.n)
                    for j in range(J):
                        ins = e.transpose(ps_x[:, j * P:(j + 1) * P], row[:, c.q, j, 0:D], ident)
                    ins.then_inc(h2_turned, 1)

                def logits():
                    e.wait_ge(h2t_ready, c.n + 1)
                    e.wait_ge(c_ready, min(c.n + 4, NCH) if c.static() else c.n + 4)
                    for j in range(J):
                        ins = e.matmul(ps_1[:, j * E:(j + 1) * E], h2t[:, j * P:(j + 1) * P], wr[:, :],
                                       start=True, stop=True)
                    ins.then_inc(logits_ready, 1)

                def ranks():
                    e.wait_ge(oh_ready, c.n + 1)
                    e.wait_ge(x1_ready, min(c.n + 2, NCH) if c.static() else c.n + 2)
                    for j in range(J):
                        for i in range(j):
                            e.matmul(ps_x[:, j * E:(j + 1) * E], ones_bf[:, :], oh[:, i, :], start=(i == 0), stop=False)
                        e.matmul(ps_x[:, j * E:(j + 1) * E], tri[:, :], oh[:, j, :], start=(j == 0), stop=True)
                    for j in range(J):
                        ins = e.matmul(ps_x[:, 64:64 + E], ones_bf[:, :], oh[:, j, :], start=(j == 0), stop=(j == J - 1))
                    ins.then_inc(counts_ready, 1)
                return ([(i, lambda i=i: rep(i)) for i in range(NG)]
                        + [((12, 16, 20, 22)[k], lambda k=k: summed(k)) for k in range(NK)]
                        + [(-31, turn), (-29, z1), (-27, z2), (-21.5, z3), (-19, z4), (-17, z5), (-13, zb), (-12, zc), (-9, s),
                           (25, turn_o), (39, turn_h2), (41, logits), (46, ranks)])
            pipeline(e, chunk_steps, once=[(-32, columns), (-22, lambda: e.wait_ge(setup_v, 3))]
                     + [(-26.3 + 0.5 * b, lambda b=b: rows_of(b)) for b in range(B)], **CHUNKS)

            def tile_steps(t):
                def turn():
                    e.wait_ge(xs_here[t.q], 16 * (t.round + 1))
                    if t.has(2):
                        e.wait_ge(xst_ready, t.n - 1)
                    e.transpose(ps_d[t.q % 2][:, 0:P], xs[:, t.q, 0:D], ident).then_inc(xs_turned, 1)

                def first():
                    e.wait_ge(xst_ready, t.n + 1)
                    e.wait_ge(w1s_ready, t.n + 1)
                    if t.has(2):
                        e.wait_ge(hid_ready, t.n - 1)
                    for f in range(FC):
                        ins = e.matmul((ps_0, ps_1)[t.q % 2][:, f * P:(f + 1) * P],
                                       w1s[:, t.q % 4, f * P:(f + 1) * P], xst[:, t.q % 2, :], start=True, stop=True)
                    ins.then_inc(hid_psum, 1)

                def second():
                    e.wait_ge(hid_ready, t.n + 1)
                    e.wait_ge(w2s_ready, t.n + 1)
                    if t.has(4):
                        e.wait_ge(v_y, 2 * t.n - 7)
                    for f in range(FC):
                        ins = e.matmul(y_banks[t.q % 4][:, 0:D], hid[:, t.q % 2, f, :], w2s[:, t.q % 4, f, :],
                                       start=(f == 0), stop=(f == FC - 1))
                    ins.then_inc(y_psum, 1)
                return [(-4, turn), (0, first), (5, second)]
            pipeline(e, tile_steps, **TILES)

        @block.vector
        def _(e):
            steps = [0]

            def then(ins):
                steps[0] += 1
                ins.then_inc(setup_chain, 1)
                e.wait_ge(setup_chain, steps[0])

            def silu():
                e.wait_ge(w_in, 16 * N_W)
                e.wait_ge(setup_a, 1)
                then(e.tensor_scalar(c_work[:, 1, :], c_work[:, 0, :], 1.0, None, ALU.add))
                then(e.reciprocal(c_work[:, 2, :], c_work[:, 1, :]))
                then(e.tensor_tensor(sc[:, :], ct[:, :], c_work[:, 2, :], ALU.mult))
                e.memset(ones[:, :], 1.0)
                e.tensor_copy(sc_rep[:, :, :], sc[:, :].unsqueeze(2).broadcast_to([P, B, P])).then_inc(setup_v, 1)

            def clamped(g, absolute, sign):
                return [
                    lambda: then(e.scalar_tensor_tensor(out=absolute, in0=g, scalar=-1.0, in1=g, op0=ALU.mult,
                                                        op1=ALU.max)),
                    lambda: then(e.tensor_scalar(absolute, absolute, 0.25, None, ALU.max)),
                    lambda: then(e.tensor_scalar(sign, g, 0.0, 2.0, ALU.is_ge, ALU.mult)),
                    lambda: then(e.tensor_scalar(sign, sign, -1.0, None, ALU.add)),
                    lambda: then(e.tensor_tensor(g, sign, absolute, ALU.mult))]

            def columns():
                e.wait_ge(setup_p, 1)
                e.tensor_tensor(bf1_all[:, :], ps_x[:, 3 * B:3 * B + 1], bf1, ALU.add)
                then(e.tensor_copy(mod_t[:, :, :], ps_x[:, 0:3 * B].rearrange("p (s b) -> p s b", b=B)))
                e.tensor_scalar(mod_t[:, 1, :], mod_t[:, 1, :], 1.0, None, ALU.add).then_inc(setup_v, 1)

            def constants():
                e.tensor_scalar(wf1_neg2[:, :], wf1[:, 1, :], -2.0, None, ALU.mult)
                e.tensor_copy(w2r[:, :, :], w23[:, 0, :].unsqueeze(2).broadcast_to([P, N, DG]))
                e.tensor_copy(w3r[:, :, :], w23[:, 1, :].unsqueeze(2).broadcast_to([P, N, DG]))
                e.memset(eighth[:, :], 1.0 / DG)
                e.tensor_copy(sel[:, :, :].rearrange("p k m -> p (k m)"), consts[0:96, C_SEL:C_SEL + NK * P])
                e.tensor_tensor(hsel[:, :, :], consts[:, C_MASK:C_MASK + MASKED].rearrange("p (g m) -> p g m", m=32),
                                h0_r.unsqueeze(2).broadcast_to([P, NQ * NK, 32]), ALU.mult)
                e.tensor_scalar(a_neg[:, :], a_r, 0.0, None, ALU.min)
                e.tensor_scalar(a_pos[:, :], a_r, 0.0, None, ALU.max)
                e.memset(ones_bf[:, :], 1.0)
                e.tensor_copy(tri[:, :], consts[:, C_TRI:C_TRI + P])
                e.tensor_copy(tok[:, :], consts[:, C_TOK:C_TOK + J])
                e.tensor_copy(base[:, 0, :], consts[:, C_BASE:C_BASE + E]).then_inc(setup_v, 1)
                e.wait_ge(setup_v, 3)

            def padding():
                e.memset(pad[:, 0:ROW - 1], 0.0)
                e.memset(pad[:, ROW - 1:ROW].bitcast(U32), NO_TOKEN).then_inc(pad_ready, 1)

            def rows_of(b):
                e.wait_ge(setup_p, b + 2)
                e.tensor_copy(mod_r[:, b, :, :].rearrange("p s d -> p (s d)"), (ps_o, ps_x)[b % 2][:, 0:3 * D])\
                    .then_inc(setup_g, 1)

            def rows_plus_1():
                e.wait_ge(setup_g, B)
                then(e.tensor_scalar(mod_r[:, :, 1, :], mod_r[:, :, 1, :], 1.0, None, ALU.add))
            setup = ([(-32.5, silu), (-31.5, columns), (-29, constants), (-28, padding)]
                     + [(-26 + 0.5 * b, lambda b=b: rows_of(b)) for b in range(B)]
                     + [(-21 + 0.1 * i, step) for i, step in
                        enumerate(clamped(mod_t[:, 2, :], mod_g[:, 0, :], mod_g[:, 1, :]))]
                     + [(-8, rows_plus_1)]
                     + [(-7.5 + i, step) for i, step in
                        enumerate(clamped(mod_r[:, :, 2, :], *(g_work[:, i, :].rearrange("p (b d) -> p b d", b=B)
                                                               for i in range(2))))])

            def norm_steps(c, src, st, m, v, w, own, ready, rstd, first, before, done, slots):
                def stats_():
                    before()
                    for j in range(J):
                        ins = e.bn_stats(st[:, j, :], src(j))
                    ins.then_inc(own, 1)

                def sums():
                    e.wait_ge(own, 5 * c.n + 1)
                    e.tensor_tensor(m[:, 0, :], st[:, :, 1], st[:, :, 4], ALU.add)
                    e.tensor_tensor(m[:, 1, :], st[:, :, 1], st[:, :, 4], ALU.subtract)
                    e.tensor_tensor(m[:, 2, :], st[:, :, 2], st[:, :, 5], ALU.add).then_inc(own, 1)

                def moments():
                    e.wait_ge(own, 5 * c.n + 2)
                    e.tensor_tensor(m[:, 3, :], m[:, 1, :], m[:, 1, :], ALU.mult)
                    e.tensor_scalar(m[:, 4, :], m[:, 2, :], 1.0 / D, EPS, ALU.mult, ALU.add)
                    e.tensor_scalar(m[:, 5, :], m[:, 0, :], 0.5, None, ALU.mult).then_inc(own, 1)

                def variance():
                    e.wait_ge(own, 5 * c.n + 3)
                    e.scalar_tensor_tensor(out=v[:, :], in0=m[:, 3, :], scalar=0.25, in1=m[:, 4, :],
                                           op0=ALU.mult, op1=ALU.add).then_inc(ready, 1)

                def newton_1():
                    e.wait_ge(rstd, c.n + 1)
                    e.tensor_tensor(w[:, 0, :], first[:, :], first[:, :], ALU.mult).then_inc(own, 1)

                def newton_2():
                    e.wait_ge(own, 5 * c.n + 4)
                    e.scalar_tensor_tensor(out=w[:, 1, :], in0=w[:, 0, :], scalar=-0.5, in1=v[:, :],
                                           op0=ALU.mult, op1=ALU.mult).then_inc(own, 1)

                def newton_3():
                    e.wait_ge(own, 5 * c.n + 5)
                    e.scalar_tensor_tensor(out=w[:, 2, :], in0=w[:, 1, :], scalar=1.5, in1=first[:, :],
                                           op0=ALU.add, op1=ALU.mult).then_inc(done, 1)

                return list(zip(slots, (stats_, sums, moments, variance, newton_1, newton_2, newton_3)))

            def chunk_steps(c):
                norm1 = norm_steps(
                    c, lambda j: x_of(c, j), stats, mv, ve, nw, v_norm, var_ready, rstd_ready, r0,
                    before=lambda: e.wait_ge(x_here[min(c.n, 2) if c.static() else 2], 16),
                    done=rstd_done, slots=(-42, -41, -40, -39, -36, -35, -34))

                def normed():
                    e.wait_ge(rstd_done, c.n + 1)
                    e.wait_ge(xn_turned, c.n)
                    for j in range(J):
                        ins = e.tensor_scalar(xn[:, j, :], x_of(c, j), mv[:, 5, j:j + 1], nw[:, 2, j:j + 1],
                                              ALU.subtract, ALU.mult)
                    ins.then_inc(xn_ready, 1)

                def tanh_in():
                    e.wait_ge(z2_ready, c.n + 1)
                    e.tensor_scalar(th[:, 0, :], ps_0[:, :], bl2, TANH_CLAMP, ALU.add, ALU.min)\
                        .then_inc(tanh_arg, 1)

                def softplus_in():
                    e.wait_ge(z5_ready, c.n + 1)
                    e.tensor_scalar(sp[:, 0, :], ps_1[:, :], b1, SOFTPLUS_CLAMP, ALU.add, ALU.min)\
                        .then_inc(sp_arg, 1)

                def softplus_out():
                    e.wait_ge(sp_log, c.n + 1)
                    e.wait_ge(dx_ready, c.n)
                    e.scalar_tensor_tensor(out=delta[:, :], in0=ps_1[:, :], scalar=b1, in1=sp[:, 0, :],
                                           op0=ALU.add, op1=ALU.max).then_inc(delta_ready, 1)

                def rest_():
                    e.wait_ge(part0_ready, c.n + 1)
                    e.tensor_tensor(rest[:, :], delta[:, :], part[:, 0, :], ALU.subtract).then_inc(v_split, 1)

                def part_1():
                    e.wait_ge(v_split, 2 * c.n + 1)
                    e.tensor_copy(part[:, 1, :], rest[:, :]).then_inc(v_split, 1)

                def part_2():
                    e.wait_ge(v_split, 2 * c.n + 2)
                    e.tensor_tensor(part[:, 2, :], rest[:, :], part[:, 1, :], ALU.subtract)\
                        .then_inc(parts_ready, 1)

                def cb_():
                    e.wait_ge(zb_ready, c.n + 1)
                    e.wait_ge(c_ready, c.n + 1)
                    e.wait_ge(s_ready, c.n)
                    e.scalar_tensor_tensor(out=cb[:, :], in0=ps_2[:, :], scalar=b2r, in1=crep[:, c.q, :],
                                           op0=ALU.add, op1=ALU.mult).then_inc(cb_ready, 1)

                def second_term():
                    e.wait_ge(dx_ready, c.n + 1)
                    e.wait_ge(s_ready, c.n + 1)
                    if c.has(2):
                        e.wait_ge(o_ready, c.n - 1)
                    e.scalar_tensor_tensor(out=y2[:, c.q, :], in0=ps_2[:, :], scalar=mod_col(2, c), in1=dx[:, :],
                                           op0=ALU.mult, op1=ALU.mult).then_inc(y2_ready, 1)

                def arg(i):
                    k, qd = i // NQ, i % NQ
                    g = NK * qd + k
                    e.wait_ge(e_ready, NG * c.n + i + 1)
                    e.scalar_tensor_tensor(out=u[:, k, qd, :], in0=ps_d[bank(i)][:, :], scalar=a_pos[:, g:g + 1],
                                           in1=u[:, k, qd, :], op0=ALU.mult, op1=ALU.add).then_inc(arg_ready, 1)

                def weighed(k):
                    e.wait_ge(g_ready, NK * c.n + k + 1)
                    e.tensor_tensor(u[:, k, :, :], u[:, k, :, :],
                                    crep[:, c.q, :].unsqueeze(1).broadcast_to([P, NQ, CH]), ALU.mult)\
                        .then_inc(w_dve, 1)

                def first_term():
                    e.wait_ge(n_summed, NK * (c.n + 1))
                    e.wait_ge(y2_ready, c.n + 1)
                    e.wait_ge(o_turned, c.n)
                    e.scalar_tensor_tensor(out=o[:, :], in0=ps_o[:, :], scalar=mod_col(2, c), in1=y2[:, c.q, :],
                                           op0=ALU.mult, op1=ALU.add).then_inc(o_ready, 1)

                def mod_copy():
                    if c.q == 0:
                        e.wait_ge(h2_ready, c.n)
                        e.tensor_copy(mod_c[:, :, :], mod_r[:, bass.ds(c.round, 1), 0:2, :]
                                      .rearrange("p o s d -> p (o s) d"))

                norm2 = norm_steps(
                    c, lambda j: row[:, c.q, j, D:2 * D], stats2, mv2, ve2, nw2, v_norm2, var2_ready,
                    rstd2_ready, r02, before=lambda: e.wait_ge(x1_ready, c.n + 1),
                    done=rstd2_done, slots=(27, 28, 29, 30, 33, 34, 35))

                def shift():
                    e.wait_ge(rstd2_done, c.n + 1)
                    e.scalar_tensor_tensor(out=nw2[:, 3, :], in0=mv2[:, 5, :], scalar=-1.0, in1=nw2[:, 2, :],
                                           op0=ALU.mult, op1=ALU.mult).then_inc(shift_ready, 1)

                def logit():
                    e.wait_ge(logits_ready, c.n + 1)
                    e.tensor_tensor(lg[:, :, :], ps_1[:, 0:J * E].rearrange("p (j e) -> p j e", e=E),
                                    br[:, :].unsqueeze(1).broadcast_to([P, J, E]), ALU.add).then_inc(logits_read, 1)

                def largest():
                    e.wait_ge(logits_read, c.n + 1)
                    e.tensor_reduce(mx[:, :], lg[:, :, :], AX.X, ALU.max).then_inc(v_route, 1)

                def compare():
                    e.wait_ge(v_route, 5 * c.n + 1)
                    e.tensor_tensor(df[:, :, :], lg[:, :, :], mx[:, :].unsqueeze(2).broadcast_to([P, J, E]),
                                    ALU.subtract).then_inc(diff_ready, 1)

                def score_():
                    e.wait_ge(diff_ready, c.n + 1)
                    e.scalar_tensor_tensor(out=score[:, :, :], in0=df[:, :, :], scalar=0.0,
                                           in1=consts[:, C_PRI:C_PRI + J * E].rearrange("p (j e) -> p j e", e=E),
                                           op0=ALU.is_ge, op1=ALU.mult).then_inc(v_route, 1)

                def best():
                    e.wait_ge(v_route, 5 * c.n + 2)
                    e.tensor_reduce(ms[:, :], score[:, :, :], AX.X, ALU.max).then_inc(v_route, 1)

                def choice():
                    e.wait_ge(v_route, 5 * c.n + 3)
                    if c.has(1):
                        e.wait_ge(counts_ready, c.n)
                        e.wait_ge(v_place, 3 * c.n - 1)
                    e.tensor_tensor(oh[:, :, :], score[:, :, :], ms[:, :].unsqueeze(2).broadcast_to([P, J, E]),
                                    ALU.is_equal).then_inc(oh_ready, 1)

                def denominator():
                    e.wait_ge(ex_ready, c.n + 1)
                    e.tensor_reduce(se[:, :], ex[:, :, :], AX.X, ALU.add).then_inc(v_route, 1)

                def gate_():
                    e.wait_ge(v_route, 5 * c.n + 4)
                    e.reciprocal(gate[:, :], se[:, :]).then_inc(v_route, 1)

                def gate_rows():
                    e.wait_ge(v_route, 5 * c.n + 5)
                    e.tensor_tensor(row[:, c.q, :, 2 * D:3 * D],
                                    mod_r[:, bass.ds(c.round, 1), 2, :].broadcast_to([P, J, D]),
                                    gate[:, :].unsqueeze(2).broadcast_to([P, J, D]), ALU.mult)
                    e.tensor_copy(row[:, c.q, :, ROW - 1:ROW].bitcast(U32).rearrange("p j o -> p (j o)"), tok[:, :])\
                        .then_inc(v_place, 1)

                def next_tokens():
                    e.wait_ge(v_place, 3 * c.n + 1)
                    e.tensor_scalar(tok[:, :], tok[:, :], float(CH), None, ALU.add).then_inc(tok_next, 1)

                def place_1():
                    e.wait_ge(counts_ready, c.n + 1)
                    e.wait_ge(base_ready, c.n)
                    e.wait_ge(ranks_read, c.n)
                    e.tensor_tensor(base[:, 1 - c.q, :], base[:, c.q, :], ps_x[:, 64:64 + E], ALU.add)\
                        .then_inc(base_ready, 1)
                    e.tensor_tensor(pos[:, :, :], base[:, c.q, :].unsqueeze(1).broadcast_to([P, J, E]),
                                    ps_x[:, 0:J * E].rearrange("p (j e) -> p j e", e=E),
                                    ALU.add).then_inc(ranks_read, 1)

                def place_2():
                    e.wait_ge(ranks_read, c.n + 1)
                    e.tensor_tensor(picked[:, :, :], pos[:, :, :], oh[:, :, :], ALU.mult).then_inc(v_place, 1)

                def place_3():
                    e.wait_ge(v_place, 3 * c.n + 2)
                    e.tensor_reduce(slotf[:, :], picked[:, :, :], AX.X, ALU.add).then_inc(v_place, 1)

                def place_4():
                    e.wait_ge(v_place, 3 * c.n + 3)
                    e.wait_ge(tok_next, c.n + 1)
                    e.tensor_copy(slot[:, c.q, :], slotf[:, :]).then_inc(row_ready, 1)

                return ([(i + 2, lambda i=i: arg(i)) for i in range(NG)] + norm1 + norm2
                        + [(NQ * k + 8, lambda k=k: weighed(k)) for k in DVE_K]
                        + [(-33, normed), (-26, tanh_in), (-16, softplus_in), (-13, softplus_out),
                           (-11, rest_), (-10, part_1), (-9, part_2), (-10, cb_),
                           (-7, second_term), (24, first_term), (26, mod_copy), (35.5, shift),
                           (42, logit), (43, largest), (43.5, compare), (44, score_), (44.5, best), (45, choice),
                           (46, denominator), (46.5, gate_), (47, gate_rows), (47.5, next_tokens),
                           (48, place_1), (48.5, place_2), (49, place_3), (49.5, place_4)])

            pipeline(e, chunk_steps, once=setup, **CHUNKS)
            e.wait_ge(row_ready, NCH)

            total = base[:, NCH % 2, :]
            then(e.tensor_tensor(cnt[:, 0, :], total, consts[:, C_BASE:C_BASE + E], ALU.subtract))
            then(e.tensor_scalar(cnt[:, 1, :], cnt[:, 0, :], 1.0 / P, (P - 1) / 2 / P, ALU.mult, ALU.add))
            then(e.tensor_scalar(cnt[:, 2, :], cnt[:, 1, :], ROUND, None, ALU.add))
            then(e.tensor_scalar(ntl[:, :], cnt[:, 2, :], ROUND, None, ALU.subtract))
            e.tensor_tensor(step[:, 0, :], total[:, 1:E], total[:, 0:E - 1], ALU.subtract)
            then(e.tensor_tensor(below[:, :, :], ntl[:, :].unsqueeze(1).broadcast_to([P, E, E]),
                                 consts[:, C_LOW:C_LOW + E * E].rearrange("p (x y) -> p x y", x=E), ALU.mult))
            then(e.tensor_reduce(cum[:, :], below[:, :, :], AX.X, ALU.add))
            e.scalar_tensor_tensor(out=step[:, 1, :], in0=ntl[:, 0:E - 1], scalar=float(P), in1=step[:, 0, :],
                                   op0=ALU.mult, op1=ALU.add)
            e.tensor_scalar(tile_w[:, 4, :], consts[:, C_TILE:C_TILE + NT], cum[:, E - 1:E], None, ALU.is_le)
            then(e.tensor_scalar(tile_w[:, 0, :], consts[:, C_TILE:C_TILE + NT], cum[:, E - 1:E], None, ALU.min))
            then(e.tensor_tensor(past[:, 0, :, :], tile_w[:, 0, :].unsqueeze(2).broadcast_to([P, NT, E - 1]),
                                 cum[:, 0:E - 1].unsqueeze(1).broadcast_to([P, NT, E - 1]), ALU.is_gt))
            e.tensor_reduce(tile_w[:, 1, :], past[:, 0, :, :], AX.X, ALU.add)
            then(e.tensor_tensor(past[:, 1, :, :], past[:, 0, :, :],
                                 step[:, 1, :].unsqueeze(1).broadcast_to([P, NT, E - 1]), ALU.mult))
            then(e.tensor_reduce(tile_w[:, 2, :], past[:, 1, :, :], AX.X, ALU.add))
            then(e.scalar_tensor_tensor(out=tile_w[:, 3, :], in0=tile_w[:, 0, :], scalar=-float(P),
                                        in1=tile_w[:, 2, :], op0=ALU.mult, op1=ALU.add))
            e.scalar_tensor_tensor(out=tile_start[:, 3:], in0=tile_w[:, 3, :], scalar=total[:, 0:1],
                                   in1=tile_w[:, 4, :], op0=ALU.add, op1=ALU.mult)
            e.tensor_copy(tile_expert[:, :], tile_w[:, 1, :]).then_inc(table_ready, 1)
            e.wait_ge(table_ready, 1)
            e.wait_ge(ffn_in, 64)
            before, expert_of = picker(e, tile_expert, 0, 2, E - 1)

            def tile_steps(t):
                def fetch():
                    x = expert_of(t)
                    if t.has(4):
                        e.wait_ge(v_y, 2 * t.n - 7)
                    e.tensor_copy(w1s[:, t.q % 4, :], ffn1[:, bass.ds(x, 1), :].rearrange("p o f -> p (o f)"))\
                        .then_inc(w1s_ready, 1)
                    if t.has(4):
                        e.wait_ge(y_psum, t.n - 3)
                    e.tensor_copy(w2s[:, t.q % 4, :, :], ffn2[:, bass.ds(x, 1), :, :].rearrange("p o f d -> p (o f) d"))\
                        .then_inc(w2s_ready, 1)

                def finish_1():
                    e.wait_ge(y_psum, t.n + 1)
                    if t.has(RING):
                        e.wait_ge(stored[t.q], 16 * t.round)
                    e.tensor_tensor(ys[:, t.q, 0, :], y_banks[t.q % 4][:, 0:D],
                                    w1s[:, t.q % 4, F + FC:W1C], ALU.add).then_inc(v_y, 1)

                def finish_2():
                    e.wait_ge(v_y, 2 * t.n + 1)
                    e.tensor_tensor(ys[:, t.q, 1, :], ys[:, t.q, 0, :], xs[:, t.q, 2 * D:3 * D], ALU.mult)\
                        .then_inc(v_y, 1)

                return [(-8, fetch), (7, finish_1), (8, finish_2)]

            pipeline(e, tile_steps, before=before, **TILES)

        @block.gpsimd
        def _(e):
            naught = e.alloc_register("naught")
            last_row = e.alloc_register("last_row")
            e.reg_mov(naught, 0)

            def chunk_steps(c):
                def weighed(k):
                    e.wait_ge(g_ready, NK * c.n + k + 1)
                    e.tensor_tensor(u[:, k, :, :], u[:, k, :, :],
                                    crep[:, c.q, :].unsqueeze(1).broadcast_to([P, NQ, CH]), ALU.mult)\
                        .then_inc(w_pool, 1)

                def dx_():
                    e.wait_ge(delta_ready, c.n + 1)
                    e.wait_ge(xt_ready, c.n + 1)
                    e.wait_ge(y2_ready, c.n)
                    e.tensor_tensor(dx[:, :], delta[:, :], xt[:, :], ALU.mult).then_inc(dx_ready, 1)

                def h2():
                    e.wait_ge(xn2_ready, c.n + 1)
                    e.tensor_tensor(hm[:, :, :], xn2[:, :, :],
                                    mod_c[:, 1, :].unsqueeze(1).broadcast_to([P, J, D]), ALU.mult)\
                        .then_inc(pool_own, 1)
                    e.wait_ge(pool_own, c.n + 1)
                    e.tensor_tensor(row[:, c.q, :, 0:D], hm[:, :, :],
                                    mod_c[:, 0, :].unsqueeze(1).broadcast_to([P, J, D]), ALU.add)\
                        .then_inc(h2_ready, 1)

                def send():
                    e.wait_ge(row_ready, c.n + 1)
                    e.wait_ge(h2_ready, c.n + 1)
                    e.reg_add(last_row, naught, E * REGION - 1)
                    for j in range(J):
                        e.indirect_dma_start(rows, bass.IndirectOffsetOnAxis(ap=slot[:, c.q, j:j + 1], axis=0),
                                             row[:, c.q, j, :], None, bounds_check=last_row,
                                             oob_is_err=True).then_inc(sent[c.q], 16)
                return [(NQ * k + 8, lambda k=k: weighed(k)) for k in POOL_K] + [(-10, dx_), (37, h2), (50, send)]
            pipeline(e, chunk_steps, **CHUNKS)

            def store(t):
                e.wait_ge(v_y, 2 * t.n + 2)
                e.tensor_tensor(ys[:, t.q, 0, :], ys[:, t.q, 1, :], xs[:, t.q, D:2 * D], ALU.add)\
                    .then_inc(y_ready, 1)
                e.wait_ge(y_ready, t.n + 1)
                e.reg_add(last_row, naught, T - 1)
                e.indirect_dma_start(out, bass.IndirectOffsetOnAxis(ap=xs[:, t.q, ROW - 1:ROW].bitcast(U32), axis=0),
                                     ys[:, t.q, 0, :], None, bounds_check=last_row, oob_is_err=False)\
                    .then_inc(stored[t.q], 16)
            pipeline(e, lambda t: [(10, lambda: store(t))], **TILES)
            for q in range(RING):
                e.wait_ge(stored[q], 16 * NT // RING)


def shape_constants(np):
    k = np.zeros((P, C_ALL), np.float32)
    p = np.arange(P)
    k[:, C_ID:C_ID + P] = np.eye(P)
    k[:, C_TRI:C_TRI + P] = p[:, None] < p[None, :]
    n, d8 = p // DG, p % DG
    for b in range(NK):
        k[0:96, C_SEL + b * P:C_SEL + (b + 1) * P] = (np.arange(96)[:, None] % 32) == (DG * b + d8)[None, :]
        for q in range(NQ):
            at = C_MASK + (NK * q + b) * 32
            k[:, at:at + 32] = np.arange(32)[None, :] == (DG * b + d8)[:, None]
    k[:, C_PRI:C_PRI + J * E] = np.tile(E - np.arange(E), J)
    k[:, C_BASE:C_BASE + E] = np.arange(E) * REGION + P
    k[:, C_TILE:C_TILE + NT] = np.arange(NT) + 1
    k[:, C_LOW:C_LOW + E * E] = np.tril(np.ones((E, E))).reshape(-1)
    k[:, C_PART] = p
    k[:, C_TOK:C_TOK + J] = p[:, None] * J + np.arange(J)
    return k


def kernel(**inputs):
    import numpy as np
    import concourse.bacc as bacc
    from concourse.bass_utils import run_bass_kernel_spmd

    v = {n: np.asarray(x) for n, x in inputs.items()}

    def by_group(m):
        return m.reshape(D // DG, DG, N).transpose(2, 1, 0).reshape(P, D // DG)

    def col(x):
        return x.reshape(-1, 1)

    smalls = np.concatenate(
        [by_group(v["L0_attn_A"]), by_group(v["L0_attn_state_init"][0]),
         col(np.repeat(v["L0_attn_b2"], DG)), col(np.repeat(v["L0_attn_b3"], DG)), col(v["L0_attn_b1"]),
         col(v["L0_attn_bl1"]), col(v["L0_attn_bl2"]), col(v["L0_attn_bf1"]), col(v["L0_attn_bf2"])], axis=1)
    arrays = {
        "x": v["L0_attn_x"].reshape(NCH, P, J * D),
        "consts": shape_constants(np),
        "smalls": smalls,
        "W1": v["L0_attn_W1"], "W2": v["L0_attn_W2"], "W3": v["L0_attn_W3"],
        "Wl1": v["L0_attn_Wl1"], "Wl2": v["L0_attn_Wl2"], "Wf1": v["L0_attn_Wf1"], "Wf2": v["L0_attn_Wf2"],
        "Wr": v["L0_ffn_Wr"], "br": v["L0_ffn_br"],
        "cT": v["L0_c"].T, "wmod": v["L0_wmod"],
        "ffn_W1": v["L0_ffn_W1"].transpose(1, 0, 2),
        "ffn_b1": v["L0_ffn_b1"].reshape(E, FC, P).transpose(2, 0, 1),
        "ffn_W2": v["L0_ffn_W2"].reshape(E, FC, P, D).transpose(2, 0, 1, 3),
        "ffn_b2": v["L0_ffn_b2"],
    }
    nc = bacc.Bacc("TRN2", target_bir_lowering=False, num_devices=1)
    arrays = {n + "_dram": np.ascontiguousarray(x) for n, x in arrays.items()}
    args = {n[:-5]: nc.dram_tensor(n, x.shape, F32, kind="ExternalInput").ap() for n, x in arrays.items()}
    out = nc.dram_tensor("out_dram", [T, D], F32, kind="ExternalOutput").ap()
    build(nc, args, out)
    r = run_bass_kernel_spmd(nc, [arrays], core_ids=[0])
    return r.results[0]["out_dram"].reshape(B, L, D)
```
